# Optimizing a Trainium2 kernel written in Bass

```python
import numpy as np
import jax
import jax.numpy as jnp

def _softmax(x, axis=-1):
    return jax.nn.softmax(x, axis=axis)

def _gelu(x):
    return jax.nn.gelu(x, approximate=True)

def _silu(x):
    return jax.nn.silu(x)

def _sigmoid(x):
    return jax.nn.sigmoid(x)

def _layernorm(x, axis=-1, eps=1e-05):
    m = jnp.mean(x, axis=axis, keepdims=True)
    v = jnp.var(x, axis=axis, keepdims=True)
    return (x - m) / jnp.sqrt(v + eps)

def _scatter_add(tgt, idx, src, axis=0):
    return tgt.at[idx].add(src)

def _segment_sum(src, seg, n):
    return jax.ops.segment_sum(src, seg, n)
kernel_name = 'mk_prb_d1_jaxref_r8_814194'

def setup_inputs(seed: int=0):
    np.random.seed(seed)
    _w = jnp.asarray

    def _L0_attn_setup():
        import jax, jax.numpy as jnp
        import numpy as np
        B, S, D, H, R = (8, 128, 128, 8, 32)
        DH = D // H

        def _lowrank(xh, U, V, b):
            t = jnp.einsum('bshd,hrd->bshr', xh, V)
            return jnp.einsum('bshr,hdr->bshd', t, U) + b
        key = jax.random.key(seed)
        ks = jax.random.split(key, 10)
        p = lambda k, shape: jax.random.normal(k, shape, dtype=jnp.float32) * 0.02
        return {'x': jax.random.normal(ks[0], (B, S, D), dtype=jnp.float32), 'Uq': p(ks[1], (H, DH, R)), 'Vq': p(ks[2], (H, R, DH)), 'bq': p(ks[3], (H, DH)), 'Uk': p(ks[4], (H, DH, R)), 'Vk': p(ks[5], (H, R, DH)), 'bk': p(ks[6], (H, DH)), 'Uv': p(ks[7], (H, DH, R)), 'Vv': p(ks[8], (H, R, DH)), 'bv': p(ks[9], (H, DH))}
    _L0_attn_in = _L0_attn_setup()

    def _L0_ffn_setup():
        import jax, jax.numpy as jnp
        import numpy as np
        H = 128
        I = 256
        E = 8
        B, S = (2, 512)
        EPS = 1e-05
        INIT = 0.02

        def _layernorm(x, w, b):
            mu = jnp.mean(x, axis=-1, keepdims=True)
            var = jnp.mean(jnp.square(x - mu), axis=-1, keepdims=True)
            return (x - mu) * jax.lax.rsqrt(var + EPS) * w + b
        key = jax.random.key(seed)
        ks = jax.random.split(key, 9)
        return {'hidden_states': jax.random.normal(ks[0], (B, S, H), jnp.float32), 'ln_w': jnp.ones((H,), jnp.float32), 'ln_b': jnp.zeros((H,), jnp.float32), 'router_w': jax.random.normal(ks[1], (H, E), jnp.float32) * INIT, 'gate_w': jax.random.normal(ks[2], (E, H, I), jnp.float32) * INIT, 'up_w': jax.random.normal(ks[3], (E, H, I), jnp.float32) * INIT, 'down_w': jax.random.normal(ks[4], (E, I, H), jnp.float32) * INIT, 'sh_gate': jax.random.normal(ks[5], (H, I), jnp.float32) * INIT, 'sh_up': jax.random.normal(ks[6], (H, I), jnp.float32) * INIT, 'sh_down': jax.random.normal(ks[7], (I, H), jnp.float32) * INIT}
    _L0_ffn_in = _L0_ffn_setup()
    _d = {'L0_attn_x': _L0_attn_in['x'], 'L0_attn_Uq': _L0_attn_in['Uq'], 'L0_attn_Vq': _L0_attn_in['Vq'], 'L0_attn_bq': _L0_attn_in['bq'], 'L0_attn_Uk': _L0_attn_in['Uk'], 'L0_attn_Vk': _L0_attn_in['Vk'], 'L0_attn_bk': _L0_attn_in['bk'], 'L0_attn_Uv': _L0_attn_in['Uv'], 'L0_attn_Vv': _L0_attn_in['Vv'], 'L0_attn_bv': _L0_attn_in['bv'], 'L0_ffn_ln_w': _L0_ffn_in['ln_w'], 'L0_ffn_ln_b': _L0_ffn_in['ln_b'], 'L0_ffn_router_w': _L0_ffn_in['router_w'], 'L0_ffn_gate_w': _L0_ffn_in['gate_w'], 'L0_ffn_up_w': _L0_ffn_in['up_w'], 'L0_ffn_down_w': _L0_ffn_in['down_w'], 'L0_ffn_sh_gate': _L0_ffn_in['sh_gate'], 'L0_ffn_sh_up': _L0_ffn_in['sh_up'], 'L0_ffn_sh_down': _L0_ffn_in['sh_down']}
    _x0 = _d['L0_attn_x']
    _d['L0_attn_x'] = jax.random.normal(jax.random.fold_in(jax.random.key(seed), 1), (4, 1024, 128), dtype=_x0.dtype)
    del _x0
    return _d

def reference(L0_attn_x, L0_attn_Uq, L0_attn_Vq, L0_attn_bq, L0_attn_Uk, L0_attn_Vk, L0_attn_bk, L0_attn_Uv, L0_attn_Vv, L0_attn_bv, L0_ffn_ln_w, L0_ffn_ln_b, L0_ffn_router_w, L0_ffn_gate_w, L0_ffn_up_w, L0_ffn_down_w, L0_ffn_sh_gate, L0_ffn_sh_up, L0_ffn_sh_down):

    def _L0_attn_ref(x, Uq, Vq, bq, Uk, Vk, bk, Uv, Vv, bv):
        import jax, jax.numpy as jnp
        import numpy as np
        B, S, D, H, R = (8, 128, 128, 8, 32)
        DH = D // H

        def _lowrank(xh, U, V, b):
            t = jnp.einsum('bshd,hrd->bshr', xh, V)
            return jnp.einsum('bshr,hdr->bshd', t, U) + b
        b_, s_, _ = x.shape
        xh = x.reshape(b_, s_, H, DH)
        q = _lowrank(xh, Uq, Vq, bq)
        k = _lowrank(xh, Uk, Vk, bk)
        v = _lowrank(xh, Uv, Vv, bv)
        scores = jnp.einsum('bqhd,bkhd->bhqk', q, k) / DH ** 0.5
        attn = jax.nn.softmax(scores, axis=-1)
        out = jnp.einsum('bhqk,bkhd->bqhd', attn, v)
        return out.reshape(b_, s_, D)

    def _L0_ffn_ref(hidden_states, ln_w, ln_b, router_w, gate_w, up_w, down_w, sh_gate, sh_up, sh_down):
        import jax, jax.numpy as jnp
        import numpy as np
        H = 128
        I = 256
        E = 8
        B, S = (2, 512)
        EPS = 1e-05
        INIT = 0.02

        def _layernorm(x, w, b):
            mu = jnp.mean(x, axis=-1, keepdims=True)
            var = jnp.mean(jnp.square(x - mu), axis=-1, keepdims=True)
            return (x - mu) * jax.lax.rsqrt(var + EPS) * w + b
        b, s, h = hidden_states.shape
        normed = _layernorm(hidden_states, ln_w, ln_b)
        xf = normed.reshape(-1, h)
        logits = xf @ router_w
        top_idx = jnp.argmax(logits, axis=-1)
        top_score = jax.nn.sigmoid(jnp.max(logits, axis=-1))

        def body(acc, ew):
            g, u, d, e = ew
            w = jnp.where(top_idx == e, top_score, 0.0)[:, None]
            xe = xf * w
            hmid = jax.nn.silu(xe @ g) * (xe @ u)
            return (acc + hmid @ d, None)
        routed, _ = jax.lax.scan(body, jnp.zeros_like(xf), (gate_w, up_w, down_w, jnp.arange(E)))
        shared = jax.nn.silu(xf @ sh_gate) * (xf @ sh_up) @ sh_down
        moe_out = (routed + shared).reshape(b, s, h)
        return hidden_states + moe_out
    x = L0_attn_x
    xn = _layernorm(x, axis=-1)
    x = x + _L0_attn_ref(xn, L0_attn_Uq, L0_attn_Vq, L0_attn_bq, L0_attn_Uk, L0_attn_Vk, L0_attn_bk, L0_attn_Uv, L0_attn_Vv, L0_attn_bv) + _L0_ffn_ref(xn, L0_ffn_ln_w, L0_ffn_ln_b, L0_ffn_router_w, L0_ffn_gate_w, L0_ffn_up_w, L0_ffn_down_w, L0_ffn_sh_gate, L0_ffn_sh_up, L0_ffn_sh_down)
    return x

_drawn_inputs = setup_inputs


def setup_inputs(seed=0):
    import zlib

    import numpy as np

    out = dict(_drawn_inputs(seed))
    spreads = {'L0_ffn_ln_w': (1.0, 0.6), 'L0_ffn_ln_b': (0.0, 0.8)}
    factors = {'L0_attn_Uq': 64.0,
     'L0_attn_Vq': 64.0,
     'L0_attn_bq': 64.0,
     'L0_attn_Uk': 64.0,
     'L0_attn_Vk': 64.0,
     'L0_attn_Uv': 64.0,
     'L0_attn_Vv': 64.0,
     'L0_attn_bv': 127.057,
     'L0_ffn_router_w': 8.0,
     'L0_ffn_gate_w': 8.0,
     'L0_ffn_up_w': 8.0,
     'L0_ffn_down_w': 8.0,
     'L0_ffn_sh_gate': 8.0,
     'L0_ffn_sh_up': 8.0,
     'L0_ffn_sh_down': 8.0,
     'L0_attn_bk': 64.0}
    for name, (base, spread) in spreads.items():
        noise = np.random.default_rng([zlib.crc32(name.encode()), seed]).standard_normal(out[name].shape)
        drawn = base * np.exp(spread * noise) if base else spread * noise
        out[name] = jnp.asarray(drawn.astype(out[name].dtype))
    for name, factor in factors.items():
        out[name] = (out[name] * factor).astype(out[name].dtype)
    return out
```

```python
import concourse.bass as bass
from concourse import mybir
from contextlib import ExitStack


def build_kernel(nc, x, UqT, Vq, bq, UkT, Vk, bk, UvT, Vv, bv, ln_w, ln_b, router_w,
                 gate_w, up_w, down_w, sh_gate, sh_up, sh_down, out):
    F32, BF16 = mybir.dt.float32, mybir.dt.bfloat16
    I32, U32 = mybir.dt.int32, mybir.dt.uint32
    ALU, ACT, AX = mybir.AluOpType, mybir.ActivationFunctionType, mybir.AxisListType
    ds = bass.ds
    nc.disable_value_cache = True

    P = 128
    B, S, D = x.shape
    H, R, DH = Vq.shape
    E, _, I = gate_w.shape
    NT, TB = B * S // P, S // P
    CH = 512
    TC = CH // P
    NCH = B * S // CH
    HG = 4
    G = H // HG
    IC = I // P
    NS = -(-(B * S + E * (P - 1)) // P)
    NS += NS % 2
    EPS, SCALE = 1e-5, float(DH) ** -0.5
    Q_PART = (0, 0, 0, 1, 1, 2)
    K_PART = (0, 1, 2, 0, 1, 0)
    NPART, NSLOT = 3, len(Q_PART)
    KR = NSLOT * DH
    KM = KR + NPART
    VM = 32
    UPB = G * 2 * TB
    QUADS = HG * TB * 2 // 4
    LEAD = 5

    split_scr = nc.dram_tensor("split_scr", [2, NPART, D, B * S], BF16, kind="Internal").ap()
    slot_x = nc.dram_tensor("slot_x", [NS * P, D], F32, kind="Internal").ap()
    slot_y = nc.dram_tensor("slot_y", [NS * P, D], F32, kind="Internal").ap()
    x_t = x.rearrange("b (t p) d -> p (b t) d", p=P)
    out_t = out.rearrange("b (t p) d -> p (b t) d", p=P)

    ctx = ExitStack()
    with ctx:
        def sb(name, shape, dt=F32):
            return ctx.enter_context(nc.sbuf_tensor(name, shape, dt))

        def sem(name):
            return ctx.enter_context(nc.semaphore(name))

        QS = sb("QS", [P, 2, H, S], BF16)
        KS = sb("KS", [P, 2, H, S], BF16)
        VALL = sb("VALL", [P, NT, H, DH + 1])
        RES = sb("RES", [P, NT, D])
        XF = sb("XF", [P, NT, D])
        XFT = sb("XFT", [P, B * S])
        U1 = sb("U1", [P, 7168])
        XN = U1[:, 0:1024].rearrange("p (s t d) -> p s t d", s=2, t=TC)
        XNT = U1[:, 1024:2048].rearrange("p (s n) -> p s n", s=2)
        QF = U1[:, 2048:4096].rearrange("p (s k n) -> p s k n", s=2, k=2)
        PARTS = U1[:, 4096:7168].bitcast(BF16).rearrange("p (s k a n) -> p s k a n", s=2, k=2, a=NPART)
        TH = U1[:, 0:1024].rearrange("p (c n) -> p c n", c=IC)
        HID = U1[:, 1024:2048].rearrange("p (c n) -> p c n", c=IC)
        PREF = U1[:, 2048:2304].rearrange("p (t e) -> p t e", t=NT)
        T128 = U1[:, 2304:2560].rearrange("p (e t) -> p e t", e=E)
        TIDX = U1[:, 2560:2560 + NS * E].rearrange("p (t e) -> p t e", t=NS)
        TOT = U1[:, 3072:3328].rearrange("p (e t) -> p e t", e=E)
        INC = U1[:, 3328:3584].rearrange("p (e t) -> p e t", e=E)
        PR = U1[:, 0:4096].rearrange("p (s j n) -> p s j n", s=4, j=2)
        VST = U1[:, 4096:6144].rearrange("p (g t j m) -> p g t j m", g=G, t=TB, j=HG)
        OSB = U1[:, 6144:6656]
        U2 = sb("U2", [P, 2304])
        ZS = U2[:, 0:1024].rearrange("p (s t d) -> p s t d", s=2, t=TC)
        XTS = U2[:, 1024:2048].rearrange("p (s n) -> p s n", s=2)
        THR = U2[:, 0:512].rearrange("p (s n) -> p s n", s=2)
        HR = U2[:, 512:1024].rearrange("p (s n) -> p s n", s=2)
        HRT = U2[:, 1024:1536].rearrange("p (s n) -> p s n", s=2)
        XS = U2[:, 1536:1792].rearrange("p (s n) -> p s n", s=2)
        XET = U2[:, 1792:2048].rearrange("p (s n) -> p s n", s=2)
        YS = U2[:, 2048:2304].rearrange("p (s n) -> p s n", s=2)
        WGU = sb("WGU", [P, E, 2 * I])
        WD = sb("WD", [P, E, IC, D])
        SHGU = sb("SHGU", [P, 2 * I])
        SHD = sb("SHD", [P, IC, D])
        RW = sb("RW", [P, E])
        FAC = sb("FAC", [P, 3, 2, G, DH])
        FACBD = sb("FACBD", [P, 3, 2, G, HG, DH])
        BLK = sb("BLK", [P, HG * DH])
        WQKV = sb("WQKV", [P, 3, D])
        BQK = sb("BQK", [P, 2])
        LNC = sb("LNC", [P, 2])
        ROWS = sb("ROWS", [P, 3, D])
        IDF = sb("IDF", [P, P])
        IDB = sb("IDB", [P, P], BF16)
        TRI = sb("TRI", [P, P])
        ONE = sb("ONE", [P, P])
        ST = sb("ST", [P, 2, TC, 6])
        MV = sb("MV", [P, 2, TC, 2])
        RSTD = sb("RSTD", [P, 2, TC])
        NHALF = sb("NHALF", [P, TC])
        LG = sb("LG", [P, NT, E])
        MXL = sb("MXL", [P, NT])
        OH = sb("OH", [P, NT, E])
        SCO = sb("SCO", [P, NT])
        ZER = sb("ZER", [P, E * NT])
        CNT = sb("CNT", [P, E])
        NTE = sb("NTE", [P, E])
        ENDT = sb("ENDT", [P, E])
        BASE = sb("BASE", [P, E])
        TEF = sb("TEF", [P, NS])
        TEI = sb("TEI", [P, NS], I32)
        DST = sb("DST", [P, NT])
        DSTI = sb("DSTI", [P, NT], U32)
        MXP = sb("MXP", [P, 2, HG * TB, 2])
        NMF = sb("NMF", [P, 2, HG * TB])
        NMP = sb("NMP", [P, 2, TB, NPART, HG], BF16)
        NMT = U1[0:NPART * HG, 6656:7168].bitcast(BF16)
        REC = sb("REC", [P, TC, HG])
        OTM = U2[:, 0:256].rearrange("p (t h d) -> p t h d", t=TC, h=HG)

        PS = ctx.enter_context(nc.psum_tensor("PS", [P, 8, CH], F32))

        x_in = [sem(f"x_in{s}") for s in range(2)]
        w_in, w2_in, consts = sem("w_in"), sem("w2_in"), sem("consts")
        fac_bd, wqkv_ps, wqkv_ready = sem("fac_bd"), sem("wqkv_ps"), sem("wqkv_ready")
        var_done, rstd_done = sem("var_done"), sem("rstd_done")
        dve_past, pool_past = sem("dve_past"), sem("pool_past")
        dve_steps, pool_steps = sem("dve_steps"), sem("pool_steps")
        xn_done, z_done, xf_done, res_done = (sem(n) for n in ("xn_done", "z_done", "xf_done", "res_done"))
        xnT_ps, xnT_ev, qkv_ps, qk_ev, v_ev = (sem(n) for n in ("xnT_ps", "xnT_ev", "qkv_ps", "qk_ev", "v_ev"))
        zT_ps, xfT_ev, lg_ps = (sem(n) for n in ("zT_ps", "xfT_ev", "lg_ps"))
        rest_done, parts_done = sem("rest_done"), sem("parts_done")
        parts_out = [sem(f"parts_out{s}") for s in range(2)]
        stack_in = sem("stack_in")
        sh_gu, sh_th, sh_h, sh_y, sh_add = (sem(n) for n in ("sh_gu", "sh_th", "sh_h", "sh_y", "sh_add"))
        mxl_done, tanh_done, score_done, oh_done, rank_ps, place_done = (sem(n) for n in (
            "mxl_done", "tanh_done", "score_done", "oh_done", "rank_ps", "place_done"))
        zero_out, scat_out = sem("zero_out"), sem("scat_out")
        xs_in = [sem(f"xs_in{s}") for s in range(2)]
        ys_out = [sem(f"ys_out{s}") for s in range(2)]
        r_xt, r_xe, r_gu, r_th, r_h, r_ht, r_hte, r_y, r_ye = (sem(n) for n in (
            "r_xt", "r_xe", "r_gu", "r_th", "r_h", "r_ht", "r_hte", "r_y", "r_ye"))
        yg_in, routed_done = sem("yg_in"), sem("routed_done")
        a_ps, a_max, nm_done, nmT_ps, nmT_ev, nm_in = (sem(n) for n in (
            "a_ps", "a_max", "nm_done", "nmT_ps", "nmT_ev", "nm_in"))
        s_ps, p_done, pv_done, o_ev, oT_ps, o_done = (sem(n) for n in (
            "s_ps", "p_done", "pv_done", "o_ev", "oT_ps", "o_done"))
        ones_done, vst_done, out_stored = sem("ones_done"), sem("vst_done"), sem("out_stored")
        block = ctx.enter_context(nc.Block())

        N_W = 14
        N_W2 = 5 + IC
        N_STACK = 2 * NSLOT
        GATE, UP = slice(0, IC), slice(IC, 2 * IC)

        class Steps:

            def __init__(self, eng, s):
                self.eng, self.sem, self.n, self.off = eng, s, 0, 0

            def done(self, ins):
                self.n += 1
                ins.then_inc(self.sem, 1)
                self.eng.wait_ge(self.sem, self.off + self.n)

            def enter(self, i, k):
                self.off, self.mark, self.k = i * k, self.n, k

            def leave(self, times):
                assert self.n - self.mark == self.k, self.n - self.mark
                self.n, self.off = self.mark + self.k * times, 0

        NM_AT = {QUADS - 1 - LEAD + 2: 1, 2 * QUADS - 1 - LEAD + 2: 2}

        def quads_of(u):
            return divmod(u + QUADS + LEAD, QUADS)

        @block.sync
        def _(sp):
            def load_x(b, s):
                t = ds(b * (2 * TC) + s * TC, TC)
                sp.dma_start(RES[:, t, :], x_t[:, t, :]).then_inc(x_in[s], 16)

            load_x(0, 0)
            load_x(0, 1)
            for k, (u, v) in enumerate(((UqT, Vq), (UkT, Vk), (UvT, Vv))):
                sp.dma_start(FAC[:, k, 0, :, :], v.rearrange("(g h) r d -> (h r) g d", g=G)).then_inc(w_in, 16)
                sp.dma_start(FAC[:, k, 1, :, :], u.rearrange("(g h) r d -> (h r) g d", g=G)).then_inc(w_in, 16)
            for k, t in enumerate((bq, bk)):
                sp.dma_start(BQK[:, k:k + 1], t.rearrange("h (d o) -> (h d) o", o=1)).then_inc(w_in, 16)
            for k, t in enumerate((ln_w, ln_b, bv.rearrange("h d -> (h d)"))):
                sp.dma_start(ROWS[:, k, :], t.partition_broadcast(P)).then_inc(w_in, 16)
            for k, t in enumerate((ln_w, ln_b)):
                sp.dma_start(LNC[:, k:k + 1], t.rearrange("(d o) -> d o", o=1)).then_inc(w_in, 16)
            sp.dma_start(RW[:, :], router_w).then_inc(w_in, 16)
            for b in range(1, B):
                for s in range(2):
                    sp.wait_ge(x_in[s], 16 * b)
                    load_x(b, s)
            sp.dma_start(SHGU[:, 0:I], sh_gate).then_inc(w2_in, 16)
            sp.dma_start(SHGU[:, I:2 * I], sh_up).then_inc(w2_in, 16)
            sp.dma_start(SHD[:, :, :], sh_down.rearrange("(c p) d -> p c d", p=P)).then_inc(w2_in, 16)
            sp.dma_start(WGU[:, :, 0:I], gate_w.rearrange("e d i -> d e i")).then_inc(w2_in, 16)
            sp.dma_start(WGU[:, :, I:2 * I], up_w.rearrange("e d i -> d e i")).then_inc(w2_in, 16)
            for c in range(IC):
                sp.dma_start(WD[:, :, c, :], down_w[:, c * P:(c + 1) * P, :].rearrange("e p d -> p e d")).then_inc(w2_in, 16)
            sp.wait_ge(consts, 1)
            zer = ZER[:, :].unsqueeze(1).to_broadcast([P, NS * D // (E * NT), E * NT])
            sp.dma_start(slot_x.rearrange("(p a) d -> p (a d)", p=P).rearrange("p (n m) -> p n m", m=E * NT), zer).then_inc(zero_out, 16)
            with sp.Fori(0, B) as b:
                for s in range(2):
                    sp.wait_ge(parts_done, b * 2 + s + 1)
                    for k in range(2):
                        sp.dma_start(split_scr[k, :, :, ds(b * S + s * CH, CH)].rearrange("a p n -> p a n"),
                                     PARTS[:, s, k]).then_inc(parts_out[s], 16)

            def load_stack(b, par):
                for slot in range(NSLOT):
                    rows = slice(slot * DH, (slot + 1) * DH)
                    for k, (T, part) in enumerate(((QS, Q_PART), (KS, K_PART))):
                        src = split_scr[k, part[slot], :, ds(b * S, S)].rearrange("(h d) t -> d h t", h=H)
                        sp.dma_start(T[rows, par, :, :], src).then_inc(stack_in, 16)

            for s in range(2):
                sp.wait_ge(parts_out[s], 16 * 2 * B)
            load_stack(0, 0)
            sp.wait_ge(stack_in, 16 * N_STACK)
            load_stack(1, 1)

            sp.wait_ge(scat_out, 16 * NT)
            with sp.Fori(0, NS // 2) as t:
                for s in range(2):
                    sp.wait_ge(r_xt, t * 2)
                    sp.dma_start(XS[:, s, :], slot_x[ds(t * (2 * P) + s * P, P), :]).then_inc(xs_in[s], 16)
                for s in range(2):
                    sp.wait_ge(r_ye, t * 2 + s + 1)
                    sp.dma_start(slot_y[ds(t * (2 * P) + s * P, P), :], YS[:, s, :]).then_inc(ys_out[s], 16)

            def nm_store(i, g, par):
                sp.wait_ge(nmT_ev, i + 1)
                for a in range(NPART):
                    sp.dma_start(QS[KR + a:KR + a + 1, par, g * HG:(g + 1) * HG, :],
                                 NMT[a * HG:(a + 1) * HG, :]).then_inc(nm_in, 16)

            def store_out(b, qh):
                sp.wait_ge(o_done, b * 4 + 3 + qh)
                t = ds(b * TB + qh * TC, TC)
                sp.dma_start(out_t[:, t, :], RES[:, t, :]).then_inc(out_stored, 16)

            def batch(b, last):
                nm_store(b * 2 + 1, 1, b % 2)
                store_out(b, 0)
                if not last:
                    nm_store(b * 2 + 2, 0, (b + 1) % 2)
                store_out(b, 1)

            nm_store(0, 0, 0)
            with sp.Fori(0, B - 2) as b:
                batch(b, False)
                sp.wait_ge(pv_done, b * UPB + UPB)
                load_stack(b + 2, b % 2)
            batch(B - 2, False)
            batch(B - 1, True)
            sp.wait_ge(out_stored, 16 * 2 * B)

        @block.gpsimd
        def _(pool):
            o = Steps(pool, pool_steps)
            nc.gpsimd.memset(ZER[:, :], 0.0).then_inc(consts, 1)
            nc.gpsimd.memset(IDF[:, :], 0.0)
            nc.gpsimd.memset(NHALF[:, :], -0.5)
            nc.gpsimd.memset(IDB[:, :], 0.0)
            o.done(nc.gpsimd.memset(ONE[:, :], 1.0))
            for m in (IDF, IDB):
                nc.gpsimd.affine_select(out=m[:, :], in_=m[:, :], compare_op=ALU.not_equal, fill=1.0,
                                        base=0, pattern=[[-1, P]], channel_multiplier=1)
            nc.gpsimd.affine_select(out=TRI[:, :], in_=ONE[:, :], compare_op=ALU.is_gt, fill=0.0,
                                    base=0, pattern=[[1, P]], channel_multiplier=-1).then_inc(consts, 1)
            pool.wait_ge(w_in, 16 * N_W)
            mask = BLK[:, :].rearrange("p (j d) -> p j d", j=HG)
            o.done(nc.gpsimd.affine_select(out=mask, in_=ONE[:, 0:HG * DH].rearrange("p (j d) -> p j d", j=HG),
                                           compare_op=ALU.is_ge, fill=0.0, base=0,
                                           pattern=[[-R, HG], [0, DH]], channel_multiplier=1))
            o.done(nc.gpsimd.affine_select(out=mask, in_=mask, compare_op=ALU.is_ge, fill=0.0, base=R - 1,
                                           pattern=[[R, HG], [0, DH]], channel_multiplier=-1))
            NF = 6 * G
            nc.gpsimd.tensor_tensor(FACBD[:, :].rearrange("p k f g j d -> p (k f g) j d"),
                                    FAC[:, :].rearrange("p k f g d -> p (k f g) d").unsqueeze(2).to_broadcast([P, NF, HG, DH]),
                                    mask.unsqueeze(1).to_broadcast([P, NF, HG, DH]), ALU.mult).then_inc(fac_bd, 1)
            nc.gpsimd.memset(VALL[:, :, :, DH:DH + 1], 1.0)
            with pool.Fori(0, B) as b:
                o.enter(b, 4)
                for k in range(4):
                    pool.wait_ge(var_done, b * 4 + k + 1)
                    nc.gpsimd.tensor_tensor(RSTD[:, k % 2, :], RSTD[:, k % 2, :], NHALF[:, :], ALU.pow).then_inc(rstd_done, 1)
                for s in range(2):
                    c = b * 2 + s
                    t = ds(b * TB + s * TC, TC)
                    pool.wait_ge(xn_done, c + 1)
                    nc.gpsimd.tensor_tensor(RES[:, t, :], RES[:, t, :], XN[:, s], ALU.add).then_inc(res_done, 1)
                    pool.wait_ge(z_done, c + 1)
                    row = lambda k: ROWS[:, k:k + 1, :].to_broadcast([P, TC, D])
                    o.done(nc.gpsimd.tensor_tensor(XF[:, t, :], ZS[:, s], row(0), ALU.mult))
                    nc.gpsimd.tensor_tensor(XF[:, t, :], XF[:, t, :], row(1), ALU.add).then_inc(xf_done, 1)
                for s in range(2):
                    pool.wait_ge(rest_done, b * 2 + s + 1)
                    pool.sem_inc(pool_past, 1)
                    o.done(nc.gpsimd.tensor_copy(PARTS[:, s, :, 1, :], QF[:, s]))
                    nc.gpsimd.tensor_tensor(PARTS[:, s, :, 2, :], QF[:, s], PARTS[:, s, :, 1, :],
                                            ALU.subtract).then_inc(parts_done, 1)
                o.leave(B)

            nc.gpsimd.iota(PREF[:, :, :], pattern=[[0, NT], [-1, E]], base=E, channel_multiplier=0,
                           allow_small_or_imprecise_dtypes=True)
            nc.gpsimd.iota(T128[:, :, :], pattern=[[0, E], [P, NT]], base=0, channel_multiplier=0,
                           allow_small_or_imprecise_dtypes=True)
            nc.gpsimd.iota(TIDX[:, :, :], pattern=[[1, NS], [0, E]], base=0, channel_multiplier=0,
                           allow_small_or_imprecise_dtypes=True).then_inc(consts, 1)

            pool.wait_ge(score_done, 1)
            o.done(nc.gpsimd.tensor_tensor(XF[:, :, :], XF[:, :, :], SCO[:, :].unsqueeze(2).to_broadcast([P, NT, D]), ALU.mult))
            pool.wait_ge(place_done, 1)
            pool.wait_ge(zero_out, 16)
            for t in range(NT):
                pool.indirect_dma_start(out=slot_x[:, :], out_offset=bass.IndirectOffsetOnAxis(ap=DSTI[:, t:t + 1], axis=0),
                                        in_=XF[:, t, :], in_offset=None).then_inc(scat_out, 16)
            for s in range(2):
                pool.wait_ge(ys_out[s], 16 * (NS // 2))
            for t in range(NT):
                pool.indirect_dma_start(out=XF[:, t, :], out_offset=None, in_=slot_y[:, :],
                                        in_offset=bass.IndirectOffsetOnAxis(ap=DSTI[:, t:t + 1], axis=0)).then_inc(yg_in, 16)
            pool.wait_ge(sh_add, NCH)
            for s in range(2):
                pool.wait_ge(parts_out[s], 16 * 2 * B)
            pool.wait_ge(v_ev, NCH)
            o.done(nc.gpsimd.memset(U1[:, 4096:6144], 0.0))

            def stage_v(b, g):
                nc.gpsimd.tensor_copy(VST[:, g, :, :, 0:DH + 1],
                                      VALL[:, ds(b * TB, TB), g * HG:(g + 1) * HG, :]).then_inc(vst_done, 1)

            stage_v(0, 0)
            stage_v(0, 1)
            pool.wait_ge(yg_in, 16 * NT)
            pool.wait_ge(sh_add, NCH)
            nc.gpsimd.tensor_tensor(RES[:, :, :], RES[:, :, :], XF[:, :, :], ALU.add).then_inc(routed_done, 1)
            with pool.Fori(0, B - 1) as b:
                for g in range(G):
                    pool.wait_ge(pv_done, b * UPB + (g + 1) * (UPB // G))
                    pool.sem_inc(pool_past, 1)
                    stage_v(b + 1, g)

        @block.scalar
        def _(act):
            act.wait_ge(consts, 1)
            nc.scalar.activation(REC[:, 0, 0:1], ZER[:, 0:1], ACT.Exp)
            act.wait_ge(w_in, 16 * N_W)
            with act.Fori(0, B) as b:
                for s in range(2):
                    c = b * 2 + s
                    act.wait_ge(xnT_ps, c + 1)
                    nc.scalar.activation(XNT[:, s, :], PS[:, 0, :], ACT.Copy).then_inc(xnT_ev, 1)
                    act.wait_ge(qkv_ps, c + 1)
                    act.wait_ge(parts_done, b * 2)
                    act.wait_ge(parts_out[s], b * 32)
                    for k in range(2):
                        nc.scalar.activation(QF[:, s, k, :], PS[:, 2 + k, :], ACT.Identity, bias=BQK[:, k:k + 1])
                        last = nc.scalar.activation(PARTS[:, s, k, 0, :], PS[:, 2 + k, :], ACT.Identity, bias=BQK[:, k:k + 1])
                    last.then_inc(qk_ev, 1)
                for s in range(2):
                    c = b * 2 + s
                    act.wait_ge(zT_ps, c + 1)
                    act.wait_ge(lg_ps, b * 2)
                    affine = dict(bias=LNC[:, 1:2], scale=LNC[:, 0:1])
                    nc.scalar.activation(XFT[:, ds(b * S + s * CH, CH)], PS[:, 1, :], ACT.Identity, **affine)
                    nc.scalar.activation(XTS[:, s, :], PS[:, 1, :], ACT.Identity, **affine).then_inc(xfT_ev, 1)
            act.wait_ge(mxl_done, 1)
            nc.scalar.activation(SCO[:, :], MXL[:, :], ACT.Tanh, scale=0.5).then_inc(tanh_done, 1)
            with act.Fori(0, NCH) as c:
                act.wait_ge(sh_gu, c + 1)
                nc.scalar.activation(TH[:, :, :], PS[:, GATE, :], ACT.Tanh, scale=0.5).then_inc(sh_th, 1)
            with act.Fori(0, NS // 2) as t:
                for s in range(2):
                    act.wait_ge(r_xt, t * 2 + s + 1)
                    nc.scalar.activation(XET[:, s, :], PS[:, 4 + s, 0:P], ACT.Copy).then_inc(r_xe, 1)
                for s in range(2):
                    act.wait_ge(r_gu, t * 2 + s + 1)
                    nc.scalar.activation(THR[:, s, :], PS[:, s, 0:I], ACT.Tanh, scale=0.5).then_inc(r_th, 1)
                for s in range(2):
                    act.wait_ge(r_ht, t * 2 + s + 1)
                    nc.scalar.activation(HRT[:, s, :], PS[:, 4 + s, P:P + I], ACT.Copy).then_inc(r_hte, 1)

            def nm_evacuate(i):
                act.wait_ge(nmT_ps, i + 1)
                act.wait_ge(nm_in, i * (16 * NPART))
                nc.scalar.activation(NMT[:, :], PS[0:NPART * HG, 7, :].bitcast(BF16), ACT.Copy).then_inc(nmT_ev, 1)

            def o_evacuate(b, j):
                o = b * 4 + j
                act.wait_ge(pv_done, (o + 1) * TB)
                act.wait_ge(oT_ps, o)
                nc.scalar.activation(OSB[:, :], PS[:, 6, :], ACT.Copy).then_inc(o_ev, 1)

            def exps(b, u):
                for hp in range(2):
                    act.wait_ge(s_ps, b * (2 * UPB) + u * 2 + hp + 1)
                    act.wait_ge(pv_done, b * UPB + max(u - 1, 0))
                    nc.scalar.activation(PR[:, (u % 2) * 2 + hp], PS[:, 2 * hp:2 * hp + 2, :], ACT.Exp,
                                         scale=SCALE).then_inc(p_done, 1)

            def batch(b, last):
                for u in range(UPB):
                    exps(b, u)
                    if u % TB == 0 and u:
                        o_evacuate(b, u // TB - 1)
                    if u in NM_AT and not (last and NM_AT[u] > 1):
                        nm_evacuate(b * 2 + NM_AT[u])
                o_evacuate(b, 2 * G - 1)

            act.wait_ge(sh_add, NCH)
            for s in range(2):
                act.wait_ge(parts_out[s], 16 * 2 * B)
            nm_evacuate(0)
            with act.Fori(0, B - 1) as b:
                batch(b, False)
            batch(B - 1, True)

        @block.vector
        def _(dve):
            o = Steps(dve, dve_steps)
            nc.vector.memset(KS[KR:KM, :, :, :], 1.0).then_inc(ones_done, 1)
            o.done(nc.vector.memset(WQKV[:, :, :], 0.0))
            dve.wait_ge(wqkv_ps, 1)
            for g in range(G):
                half = slice(g * HG * DH, (g + 1) * HG * DH)
                last = nc.vector.tensor_copy(WQKV[half, :, half],
                                             PS[half, 0, 0:3 * HG * DH].rearrange("p (k d) -> p k d", k=3))
            last.then_inc(wqkv_ready, 1)

            def moments(src, s):
                for j in range(TC):
                    last = nc.vector.bn_stats(ST[:, s, j, :], src(j))
                o.done(last)
                dve.sem_inc(dve_past, 1)
                for j in range(TC):
                    last = nc.vector.bn_aggr(MV[:, s, j, :], ST[:, s, j, :])
                o.done(last)
                nc.vector.tensor_scalar(RSTD[:, s, :], MV[:, s, :, 1], EPS, None, ALU.add).then_inc(var_done, 1)

            def normalize(src, dst, s):
                for j in range(TC):
                    last = nc.vector.tensor_scalar(dst(j), src(j), MV[:, s, j, 0:1], RSTD[:, s, j:j + 1],
                                                   ALU.subtract, ALU.mult)
                return last

            with dve.Fori(0, B) as b:
                o.enter(b, 8)
                x_tile = lambda s: lambda j: RES[:, b * TB + (s * TC + j), :]
                xn_tile = lambda s: lambda j: XN[:, s, j, :]
                for s in range(2):
                    dve.wait_ge(x_in[s], b * 16 + 16)
                    moments(x_tile(s), s)
                for s in range(2):
                    dve.wait_ge(rstd_done, b * 4 + s + 1)
                    dve.wait_ge(xnT_ps, b * 2)
                    dve.wait_ge(res_done, b * 2)
                    normalize(x_tile(s), xn_tile(s), s).then_inc(xn_done, 1)
                    dve.wait_ge(xn_done, b * 2 + s + 1)
                    moments(xn_tile(s), s)
                for s in range(2):
                    dve.wait_ge(rstd_done, b * 4 + 2 + s + 1)
                    dve.wait_ge(zT_ps, b * 2)
                    dve.wait_ge(xf_done, b * 2)
                    normalize(xn_tile(s), lambda j: ZS[:, s, j, :], s).then_inc(z_done, 1)
                for s in range(2):
                    c = b * 2 + s
                    dve.wait_ge(qk_ev, c + 1)
                    nc.vector.tensor_tensor(QF[:, s], QF[:, s], PARTS[:, s, :, 0, :], ALU.subtract).then_inc(rest_done, 1)
                    dve.wait_ge(qkv_ps, c + 1)
                    for j in range(TC):
                        last = nc.vector.tensor_tensor(
                            VALL[:, b * TB + (s * TC + j), :, 0:DH],
                            PS[:, 4 + s, j * D:(j + 1) * D].rearrange("p (h d) -> p h d", h=H),
                            ROWS[:, 2, :].rearrange("p (h d) -> p h d", h=H), ALU.add)
                    last.then_inc(v_ev, 1)
                o.leave(B)

            per_t = lambda v: v.unsqueeze(2).to_broadcast([P, NT, E])
            dve.wait_ge(lg_ps, NCH)
            dve.wait_ge(consts, 3)
            o.done(nc.vector.tensor_copy(LG[:, :, :], PS[:, 6, 0:NT * E].rearrange("p (t e) -> p t e", t=NT)))
            nc.vector.tensor_reduce(MXL[:, :], LG[:, :, :], AX.X, ALU.max).then_inc(mxl_done, 1)
            dve.wait_ge(mxl_done, 1)
            o.done(nc.vector.tensor_tensor(OH[:, :, :], LG[:, :, :], per_t(MXL[:, :]), ALU.is_equal))
            o.done(nc.vector.tensor_tensor(OH[:, :, :], OH[:, :, :], PREF[:, :, :], ALU.mult))
            o.done(nc.vector.tensor_reduce(DST[:, :], OH[:, :, :], AX.X, ALU.max))
            nc.vector.tensor_tensor(OH[:, :, :], OH[:, :, :], per_t(DST[:, :]), ALU.is_equal).then_inc(oh_done, 1)
            dve.wait_ge(tanh_done, 1)
            nc.vector.tensor_scalar(SCO[:, :], SCO[:, :], 0.5, 0.5, ALU.mult, ALU.add).then_inc(score_done, 1)
            per_e = lambda v: v.unsqueeze(2).to_broadcast([P, E, NT])
            flat = lambda T: T[:, :, :].rearrange("p a b -> p (a b)")
            dve.wait_ge(rank_ps, 1)
            o.done(nc.vector.tensor_copy(TOT[:, :, :], PS[:, 7, 0:NT * E].rearrange("p (t e) -> p e t", t=NT)))
            o.done(nc.vector.tensor_tensor_scan(flat(INC), flat(TOT), ZER[:, :], 0.0, ALU.add, ALU.add))
            o.done(nc.vector.tensor_tensor(CNT[:, :], INC[:, :, NT - 1], INC[:, :, 0], ALU.subtract))
            o.done(nc.vector.tensor_tensor(CNT[:, :], CNT[:, :], TOT[:, :, 0], ALU.add))
            more = LG[:, :, :].rearrange("p t e -> p (t e)").rearrange("p (e t) -> p e t", e=E)
            o.done(nc.vector.tensor_tensor(more, per_e(CNT[:, :]), T128[:, :, :], ALU.is_gt))
            o.done(nc.vector.tensor_reduce(NTE[:, :], more, AX.X, ALU.add))
            o.done(nc.vector.tensor_tensor_scan(ENDT[:, :], NTE[:, :], ZER[:, 0:E], 0.0, ALU.add, ALU.add))
            o.done(nc.vector.tensor_tensor(NTE[:, :], ENDT[:, :], NTE[:, :], ALU.subtract))
            o.done(nc.vector.tensor_tensor(CNT[:, :], TOT[:, :, 0], INC[:, :, 0], ALU.subtract))
            o.done(nc.vector.scalar_tensor_tensor(BASE[:, :], NTE[:, :], float(P), CNT[:, :], ALU.mult, ALU.add))
            o.done(nc.vector.tensor_tensor(INC[:, :, :], INC[:, :, :], TOT[:, :, :], ALU.subtract))
            o.done(nc.vector.tensor_tensor(INC[:, :, :], INC[:, :, :], per_e(BASE[:, :]), ALU.add))
            o.done(nc.vector.tensor_tensor(LG[:, :, :], PS[:, 6, 0:NT * E].rearrange("p (t e) -> p t e", t=NT),
                                           INC[:, :, :].rearrange("p e t -> p t e"), ALU.add))
            o.done(nc.vector.tensor_tensor(LG[:, :, :], LG[:, :, :], OH[:, :, :], ALU.mult))
            o.done(nc.vector.tensor_reduce(DST[:, :], LG[:, :, :], AX.X, ALU.add))
            nc.vector.tensor_copy(DSTI[:, :], DST[:, :])
            o.done(nc.vector.tensor_tensor(TIDX[:, :, :], TIDX[:, :, :],
                                           ENDT[:, :].unsqueeze(1).to_broadcast([P, NS, E]), ALU.is_ge))
            o.done(nc.vector.tensor_reduce(TEF[:, :], TIDX[:, :, :], AX.X, ALU.add))
            nc.vector.tensor_scalar(TEI[:, :], TEF[:, :], float(E - 1), None, ALU.min).then_inc(place_done, 1)

            dve.wait_ge(res_done, NCH)
            with dve.Fori(0, NCH) as c:
                o.enter(c, 1)
                dve.wait_ge(sh_th, c + 1)
                dve.wait_ge(sh_y, c)
                o.done(nc.vector.scalar_tensor_tensor(HID[:, :, :], TH[:, :, :], 1.0, PS[:, GATE, :], ALU.add, ALU.mult))
                nc.vector.scalar_tensor_tensor(HID[:, :, :], HID[:, :, :], 0.5, PS[:, UP, :], ALU.mult,
                                               ALU.mult).then_inc(sh_h, 1)
                dve.wait_ge(sh_y, c + 1)
                t = ds(c * TC, TC)
                nc.vector.tensor_tensor(RES[:, t, :], RES[:, t, :], PS[:, 6, :].rearrange("p (t d) -> p t d", t=TC),
                                        ALU.add).then_inc(sh_add, 1)
                o.leave(NCH)

            with dve.Fori(0, NS // 2) as t:
                o.enter(t, 2)
                for s in range(2):
                    dve.wait_ge(r_th, t * 2 + s + 1)
                    dve.wait_ge(r_ht, t * 2)
                    o.done(nc.vector.scalar_tensor_tensor(HR[:, s, :], THR[:, s, :], 1.0, PS[:, s, 0:I], ALU.add, ALU.mult))
                    nc.vector.scalar_tensor_tensor(HR[:, s, :], HR[:, s, :], 0.5, PS[:, s, I:2 * I], ALU.mult,
                                                   ALU.mult).then_inc(r_h, 1)
                for s in range(2):
                    dve.wait_ge(r_y, t * 2 + s + 1)
                    dve.wait_ge(ys_out[s], t * 16)
                    nc.vector.tensor_copy(YS[:, s, :], PS[:, 4 + s, P + I:P + I + D]).then_inc(r_ye, 1)
                o.leave(NS // 2)

            def quad(i, slot, k):
                for j in range(4):
                    dve.wait_ge(a_ps, i * (4 * QUADS) + 4 * k + j + 1)
                    row = (k // 4) * TB + 2 * (k % 4) + j // 2
                    nc.vector.tensor_reduce(MXP[:, slot, row, j % 2:j % 2 + 1], PS[:, 4 + j % 2, :], AX.X,
                                            ALU.max).then_inc(a_max, 1)

            def finalize(i, slot, first):
                dve.wait_ge(a_max, i * (4 * QUADS) + 4 * QUADS)
                o.done(nc.vector.tensor_reduce(NMF[:, slot, :], MXP[:, slot, :, :], AX.X, ALU.max, negate=True))
                if not first:
                    dve.wait_ge(nmT_ps, i - 1)
                rest = NMF[:, slot, :].rearrange("p (h t) -> p t h", h=HG)
                for a in range(NPART):
                    part = NMP[:, slot, :, a, :]
                    ins = nc.vector.tensor_copy(part, rest)
                    if a < NPART - 1:
                        o.done(ins)
                        o.done(nc.vector.tensor_tensor(rest, rest, part, ALU.subtract))
                ins.then_inc(nm_done, 1)

            def output(b, j):
                g, qh = divmod(j, 2)
                dve.wait_ge(oT_ps, b * 4 + j + 1)
                o_t = PS[:, 7, :].rearrange("p (t h m) -> p t h m", t=TC, h=HG)
                o.done(nc.vector.reciprocal(REC[:, :, :], o_t[:, :, :, DH]))
                o.done(nc.vector.tensor_tensor(OTM[:, :, :, :], o_t[:, :, :, 0:DH],
                                               REC[:, :, :].unsqueeze(3).to_broadcast([P, TC, HG, DH]), ALU.mult))
                dst = RES[:, ds(b * TB + qh * TC, TC), g * HG * DH:(g + 1) * HG * DH]
                nc.vector.tensor_tensor(dst, dst, OTM[:, :, :, :].rearrange("p t h d -> p t (h d)"),
                                        ALU.add).then_inc(o_done, 1)

            def batch(b, last):
                for u in range(UPB):
                    ahead, k = quads_of(u)
                    if not (last and ahead > 1):
                        quad(b * 2 + ahead, ahead % 2, k)
                        if k == QUADS - 1:
                            finalize(b * 2 + ahead, ahead % 2, False)
                    if u % TB == 1 and u > TB:
                        output(b, u // TB - 1)
                output(b, 2 * G - 1)

            with dve.Fori(0, HG) as h:
                for k in range(QUADS // HG):
                    for j in range(4):
                        dve.wait_ge(a_ps, h * 16 + 4 * k + j + 1)
                        nc.vector.tensor_reduce(MXP[:, 0, ds(h * TB + (2 * k + j // 2), 1), j % 2], PS[:, 4 + j % 2, :],
                                                AX.X, ALU.max).then_inc(a_max, 1)
            finalize(0, 0, True)
            for k in range(LEAD):
                quad(1, 1, k)
            dve.wait_ge(routed_done, 1)
            with dve.Fori(0, B - 1) as b:
                o.enter(b, 2 * 5 + 4 * 2)
                batch(b, False)
                o.leave(B - 1)
            batch(B - 1, True)

        @block.tensor
        def _(pe):
            mm = nc.tensor.matmul
            pe.wait_ge(fac_bd, 1)
            GD = HG * DH
            for k in range(3):
                for g in range(G):
                    last = mm(PS[g * GD:(g + 1) * GD, 0, k * GD:(k + 1) * GD],
                              FACBD[:, k, 0, g].rearrange("p j d -> p (j d)"),
                              FACBD[:, k, 1, g].rearrange("p j d -> p (j d)"), start=True, stop=True)
            last.then_inc(wqkv_ps, 1)
            pe.wait_ge(consts, 2)
            pe.wait_ge(wqkv_ready, 1)
            with pe.Fori(0, B) as b:
                for s in range(2):
                    c = b * 2 + s
                    pe.wait_ge(xn_done, c + 1)
                    for j in range(TC):
                        last = nc.tensor.transpose(PS[:, 0, j * P:(j + 1) * P], XN[:, s, j, :], IDF[:, :])
                    last.then_inc(xnT_ps, 1)
                    pe.wait_ge(xnT_ev, c + 1)
                    pe.wait_ge(qk_ev, c)
                    pe.wait_ge(v_ev, b * 2)
                    for k in range(2):
                        mm(PS[:, 2 + k, :], WQKV[:, k, :], XNT[:, s, :], start=True, stop=True)
                    for j in range(TC):
                        last = mm(PS[:, 4 + s, j * D:(j + 1) * D], XNT[:, s, j * P:(j + 1) * P], WQKV[:, 2, :],
                                  start=True, stop=True)
                    last.then_inc(qkv_ps, 1)
                for s in range(2):
                    c = b * 2 + s
                    pe.wait_ge(z_done, c + 1)
                    for j in range(TC):
                        last = nc.tensor.transpose(PS[:, 1, j * P:(j + 1) * P], ZS[:, s, j, :], IDF[:, :])
                    last.then_inc(zT_ps, 1)
                    pe.wait_ge(xfT_ev, c + 1)
                    for j in range(TC):
                        last = mm(PS[:, 6, ds(b * (TB * E) + (s * TC + j) * E, E)], XTS[:, s, j * P:(j + 1) * P], RW[:, :],
                                  start=True, stop=True)
                    last.then_inc(lg_ps, 1)

            pe.wait_ge(oh_done, 1)
            hot = OH[:, :, :].rearrange("p t e -> p (t e)")
            mm(PS[:, 6, 0:NT * E], TRI[:, :], hot, start=True, stop=True)
            mm(PS[:, 7, 0:NT * E], ONE[:, :], hot, start=True, stop=True).then_inc(rank_ps, 1)

            pe.wait_ge(w2_in, 16 * N_W2)
            pe.wait_ge(place_done, 1)
            with pe.Fori(0, NCH) as c:
                pe.wait_ge(sh_h, c)
                for j in range(2 * IC):
                    last = mm(PS[:, j, :], SHGU[:, j * P:(j + 1) * P], XFT[:, ds(c * CH, CH)], start=True, stop=True)
                last.then_inc(sh_gu, 1)
                pe.wait_ge(sh_h, c + 1)
                pe.wait_ge(sh_add, c)
                for j in range(TC):
                    for i in range(IC):
                        last = mm(PS[:, 6, j * D:(j + 1) * D], HID[:, i, j * P:(j + 1) * P], SHD[:, i, :],
                                  start=(i == 0), stop=(i == IC - 1))
                last.then_inc(sh_y, 1)

            with pe.Fori(0, NS // 2) as t:
                for s in range(2):
                    pe.wait_ge(xs_in[s], t * 16 + 16)
                    pe.wait_ge(r_ye, t * 2)
                    nc.tensor.transpose(PS[:, 4 + s, 0:P], XS[:, s, :], IDF[:, :]).then_inc(r_xt, 1)
                expert = [pe.value_load(TEI[0:1, ds(t * 2 + s, 1)], min_val=0, max_val=E - 1) for s in range(2)]
                for s in range(2):
                    pe.wait_ge(r_xe, t * 2 + s + 1)
                    pe.wait_ge(r_h, t * 2)
                    mm(PS[:, s, :], XET[:, s, :], WGU[:, expert[s], :], start=True, stop=True).then_inc(r_gu, 1)
                for s in range(2):
                    pe.wait_ge(r_h, t * 2 + s + 1)
                    for i in range(IC):
                        last = nc.tensor.transpose(PS[:, 4 + s, (1 + i) * P:(2 + i) * P], HR[:, s, i * P:(i + 1) * P], IDF[:, :])
                    last.then_inc(r_ht, 1)
                for s in range(2):
                    pe.wait_ge(r_hte, t * 2 + s + 1)
                    for i in range(IC):
                        last = mm(PS[:, 4 + s, P + I:P + I + D], HRT[:, s, i * P:(i + 1) * P], WD[:, expert[s], i, :],
                                  start=(i == 0), stop=(i == IC - 1))
                    last.then_inc(r_y, 1)

            def block_of_maxima(par, head, qt, kh):
                return mm(PS[:, 4 + kh, :], QS[0:KR, par, head, qt * P:(qt + 1) * P],
                          KS[0:KR, par, head, kh * CH:(kh + 1) * CH], start=True, stop=True)

            def quad(i, par, g, k):
                if g == 0 and k == 0:
                    pe.wait_ge(stack_in, (i // 2 + 1) * (16 * N_STACK))
                for j in range(4):
                    pe.wait_ge(a_max, i * (4 * QUADS) + (4 * k + j - 1))
                    block_of_maxima(par, g * HG + k // 4, 2 * (k % 4) + j // 2, j % 2).then_inc(a_ps, 1)

            def transpose_maxima(i, slot, outputs):
                pe.wait_ge(nm_done, i + 1)
                pe.wait_ge(o_done, outputs)
                pe.wait_ge(nmT_ev, i)
                rows = PS[0:NPART * HG, 7, :].bitcast(BF16)
                for t in range(TB):
                    last = nc.tensor.transpose(rows[:, t * P:(t + 1) * P],
                                               NMP[:, slot, t].rearrange("p a h -> p (a h)"), IDB[:, :])
                last.then_inc(nmT_ps, 1)

            def transpose_output(b, j, maxima):
                pe.wait_ge(o_ev, b * 4 + j + 1)
                pe.wait_ge(o_done, b * 4 + j)
                pe.wait_ge(nmT_ev, maxima)
                for t in range(TC):
                    last = nc.tensor.transpose(PS[:, 7, t * P:(t + 1) * P], OSB[:, t * P:(t + 1) * P], IDF[:, :])
                last.then_inc(oT_ps, 1)

            def scores(b, u):
                g, qh, kt = u // (2 * TB), u // TB % 2, u % TB
                if qh == 0 and kt == 0:
                    pe.wait_ge(nm_in, b * (2 * 16 * NPART) + (g + 1) * (16 * NPART))
                for hp in range(2):
                    if u:
                        pe.wait_ge(p_done, b * (2 * UPB) + (2 * u + hp - 1))
                    for j in range(2):
                        head = g * HG + 2 * hp + j
                        last = mm(PS[:, 2 * hp + j, :], KS[0:KM, b % 2, head, kt * P:(kt + 1) * P],
                                  QS[0:KM, b % 2, head, qh * CH:(qh + 1) * CH], start=True, stop=True)
                    last.then_inc(s_ps, 1)

            def values(b, u):
                g, qh, kt = u // (2 * TB), u // TB % 2, u % TB
                if kt == 0:
                    pe.wait_ge(o_ev, b * 4 + u // TB)
                    if qh == 0:
                        pe.wait_ge(vst_done, b * G + (g + 1))
                pe.wait_ge(p_done, b * (2 * UPB) + (2 * u + 2))
                for j in range(HG):
                    last = mm(PS[j * VM:(j + 1) * VM, 6, :], VST[:, g, kt, j, :], PR[:, (u % 2) * 2 + j // 2, j % 2, :],
                              start=(kt == 0), stop=(kt == TB - 1))
                last.then_inc(pv_done, 1)

            def batch(b, last):
                scores(b, 0)
                for u in range(UPB):
                    if u + 1 < UPB:
                        scores(b, u + 1)
                    ahead, k = quads_of(u)
                    if not (last and ahead > 1):
                        quad(b * 2 + ahead, (b + ahead // 2) % 2, ahead % 2, k)
                    values(b, u)
                    if u % TB == 0 and u:
                        j = u // TB - 1
                        transpose_output(b, j, b * 2 + (1 if j == 0 else 2))
                    if u in NM_AT and not (last and NM_AT[u] > 1):
                        a = NM_AT[u]
                        transpose_maxima(b * 2 + a, a % 2, b * 4 + (1 if a == 1 else 3))
                transpose_output(b, 3, b * 2 + (2 if last else 3))

            pe.wait_ge(r_ye, NS)
            pe.wait_ge(sh_add, NCH)
            pe.wait_ge(ones_done, 1)
            pe.wait_ge(stack_in, 16 * N_STACK)
            with pe.Fori(0, HG) as h:
                for k in range(QUADS // HG):
                    for j in range(4):
                        pe.wait_ge(a_max, h * 16 + max(4 * k + j - 1, 0))
                        block_of_maxima(0, h, 2 * k + j // 2, j % 2).then_inc(a_ps, 1)
            transpose_maxima(0, 0, 0)
            for k in range(LEAD):
                quad(1, 0, 1, k)
            with pe.Fori(0, B - 1) as b:
                batch(b, False)
            batch(B - 1, True)


_INS = ["x", "Uq", "Vq", "bq", "Uk", "Vk", "bk", "Uv", "Vv", "bv", "ln_w", "ln_b", "router_w",
        "gate_w", "up_w", "down_w", "sh_gate", "sh_up", "sh_down"]


def kernel(**inputs):
    import numpy as _np
    import concourse.bacc as _bacc
    from concourse import mybir as _mybir
    from concourse.bass_utils import run_bass_kernel_spmd as _run

    nc = _bacc.Bacc("TRN2", target_bir_lowering=False, num_devices=1)
    arrays, args = {}, []
    for name in _INS:
        full = next(k for k in inputs if k in (f"L0_attn_{name}", f"L0_ffn_{name}"))
        a = _np.asarray(inputs[full])
        if name in ("Uq", "Uk", "Uv"):
            a = a.transpose(0, 2, 1)
        a = _np.ascontiguousarray(a)
        arrays[f"in_{name}_dram"] = a
        args.append(nc.dram_tensor(f"in_{name}_dram", a.shape, _mybir.dt.from_np(a.dtype), kind="ExternalInput").ap())
    dt = _mybir.dt.from_np(_np.dtype("float32"))
    args.append(nc.dram_tensor("out_0_dram", (4, 1024, 128), dt, kind="ExternalOutput").ap())
    build_kernel(nc, *args)
    r = _run(nc, [arrays], core_ids=[0])
    return r.results[0]["out_0_dram"]
```

```python
import concourse.bass as bass
from concourse import mybir
from contextlib import ExitStack


def build_kernel(nc, x, UqT, Vq, bq, UkT, Vk, bk, UvT, Vv, bv, ln_w, ln_b, router_w,
                 gate_w, up_w, down_w, sh_gate, sh_up, sh_down, out):
    F32, BF16 = mybir.dt.float32, mybir.dt.bfloat16
    I32, U32 = mybir.dt.int32, mybir.dt.uint32
    ALU, ACT, AX = mybir.AluOpType, mybir.ActivationFunctionType, mybir.AxisListType
    ds = bass.ds
    nc.disable_value_cache = True

    P = 128
    B, S, D = x.shape
    H, R, DH = Vq.shape
    E, _, I = gate_w.shape
    NT, TB = B * S // P, S // P
    CH = 512
    TC = CH // P
    NCH = B * S // CH
    HG = 4
    G = H // HG
    IC = I // P
    NS = -(-(B * S + E * (P - 1)) // P)
    EPS, SCALE = 1e-5, float(DH) ** -0.5
    Q_PART = (0, 0, 0, 1, 1, 2)
    K_PART = (0, 1, 2, 0, 1, 0)
    NPART, NSLOT = 3, len(Q_PART)
    KR = NSLOT * DH
    KM = KR + NPART
    VM = 32
    UPB = G * 2 * TB
    QUADS = HG * TB * 2 // 4
    LEAD = 5
    ROW = D + 2

    TILE_AT = (1, 9, 17, 25, 37, 45, 57, 69, 77, 85, 101, 109)
    STAGES = {"yx": 0, "gu": 2, "ht": 6}
    HID_AFTER = 2
    OUT_AT = (35, 67, 99, 1000)
    NM_AT = {4 * (QUADS - LEAD + 2) + 1: 1, 4 * (2 * QUADS - LEAD + 2) + 1: 2}
    PRE_AT, PRE_GAPS = (1, 6, 11, 16), 22
    PRE_STAGES = {"yx": 0, "gu": 1, "ht": 4}
    NPRE, NTB = len(PRE_AT), len(TILE_AT)
    NBT = -(-(NS - NPRE) // NTB)
    NS = NPRE + NBT * NTB
    assert NBT == B - 1 and NPRE % 2 == 0 and NTB % 2 == 0

    def uses(tile_at, stages, nm_at, out_at):
        found = [(n + d, kind, k) for k, n in enumerate(tile_at) for kind, d in stages.items()]
        found += [(n, "nm", a) for n, a in nm_at.items()] + [(n, "out", j) for j, n in enumerate(out_at)]
        found.sort()
        assert len({n for n, _, _ in found}) == len(found)
        return {n: (kind, k) for n, kind, k in found}, {(kind, k): i for i, (_, kind, k) in enumerate(found)}

    PRE_USE, PRE_IX = uses(PRE_AT, PRE_STAGES, {0: 0}, ())
    BAT_USE, BAT_IX = uses(TILE_AT, STAGES, NM_AT, OUT_AT)
    END_USE, END_IX = uses(TILE_AT[:1], {"yx": 0}, {n: a for n, a in NM_AT.items() if a == 1}, OUT_AT)

    split_scr = nc.dram_tensor("split_scr", [2, NPART, D, B * S], BF16, kind="Internal").ap()
    slot_x = nc.dram_tensor("slot_x", [(NS + 2) * P, ROW], F32, kind="Internal").ap()
    slot_y = nc.dram_tensor("slot_y", [NS * P, D], F32, kind="Internal").ap()
    x_t = x.rearrange("b (t p) d -> p (b t) d", p=P)
    out_t = out.rearrange("b (t p) d -> p (b t) d", p=P)

    ctx = ExitStack()
    with ctx:
        def sb(name, shape, dt=F32):
            return ctx.enter_context(nc.sbuf_tensor(name, shape, dt))

        def sem(name):
            return ctx.enter_context(nc.semaphore(name))

        QS = sb("QS", [P, 2, H, S], BF16)
        KS = sb("KS", [P, 2, H, S], BF16)
        VALL = sb("VALL", [P, NT, H, DH + 1])
        RES = sb("RES", [P, NT, D])
        ZALL = sb("ZALL", [P, NT, ROW])
        XFT = sb("XFT", [P, B * S])
        U1 = sb("U1", [P, 7168])
        XN = U1[:, 0:1024].rearrange("p (s t d) -> p s t d", s=2, t=TC)
        XNT = U1[:, 1024:2048].rearrange("p (s n) -> p s n", s=2)
        QF = U1[:, 2048:4096].rearrange("p (s k n) -> p s k n", s=2, k=2)
        PARTS = U1[:, 4096:7168].bitcast(BF16).rearrange("p (s k a n) -> p s k a n", s=2, k=2, a=NPART)
        TH = U1[:, 0:1024].rearrange("p (c n) -> p c n", c=IC)
        HID = U1[:, 1024:3072].rearrange("p (s c n) -> p s c n", s=2, c=IC)
        PREF = U1[:, 2048:2304].rearrange("p (t e) -> p t e", t=NT)
        T128 = U1[:, 2304:2560].rearrange("p (e t) -> p e t", e=E)
        TIDX = U1[:, 2560:2560 + NS * E].rearrange("p (t e) -> p t e", t=NS)
        TOT = U1[:, 3072:3328].rearrange("p (e t) -> p e t", e=E)
        INC = U1[:, 3328:3584].rearrange("p (e t) -> p e t", e=E)
        PR = U1[:, 0:4096].rearrange("p (s j n) -> p s j n", s=4, j=2)
        VST = U1[:, 4096:6144].rearrange("p (g t j m) -> p g t j m", g=G, t=TB, j=HG)
        OSB = U1[:, 6144:6656]
        U2 = sb("U2", [P, 2308 + 256])
        FACBD = U2[:, 0:6 * G * HG * DH].rearrange(
            "p (k f g j d) -> p k f g j d", k=3, f=2, g=G, j=HG)
        ZS = U2[:, 0:1024].rearrange("p (s t d) -> p s t d", s=2, t=TC)
        XTS = U2[:, 1024:2048].rearrange("p (s n) -> p s n", s=2)
        THR = U2[:, 0:512].rearrange("p (s n) -> p s n", s=2)
        HR = U2[:, 512:1024].rearrange("p (s n) -> p s n", s=2)
        HRT = U2[:, 1024:1536].rearrange("p (s n) -> p s n", s=2)
        XS = U2[:, 2304:2304 + 2 * ROW].rearrange("p (s n) -> p s n", s=2)
        XET = U2[:, 1792:2048].rearrange("p (s n) -> p s n", s=2)
        OTM = U2[:, 1536:1792].rearrange("p (t h d) -> p t h d", t=TC, h=HG)
        YS = U2[:, 2048:2304].rearrange("p (s n) -> p s n", s=2)
        WGU = sb("WGU", [P, E, 2 * I])
        WD = sb("WD", [P, E, IC, D])
        SHGU = sb("SHGU", [P, 2 * I])
        SHD = sb("SHD", [P, IC, D])
        RW = sb("RW", [P, E])
        FAC = sb("FAC", [P, 3, 2, G, DH])
        BLK = sb("BLK", [P, HG * DH])
        WQKV = sb("WQKV", [P, 3, D])
        BQK = sb("BQK", [P, 2])
        LNC = sb("LNC", [P, 2])
        BVR = sb("BVR", [P, D])
        IDF = sb("IDF", [P, P])
        IDB = sb("IDB", [P, P], BF16)
        TRI = sb("TRI", [P, P])
        ONE = sb("ONE", [P, P])
        ONEB = sb("ONEB", [NPART, P], BF16)
        ST = sb("ST", [P, 2, TC, 6])
        MV = sb("MV", [P, 2, TC, 2])
        RSTD = sb("RSTD", [P, 2, TC])
        NHALF = sb("NHALF", [P, TC])
        LG = sb("LG", [P, NT, E])
        MXL = sb("MXL", [P, NT])
        OH = sb("OH", [P, NT, E])
        SCO = sb("SCO", [P, 2, NT])
        ZER = sb("ZER", [P, E * NT])
        CNT = sb("CNT", [P, E])
        NTE = sb("NTE", [P, E])
        ENDT = sb("ENDT", [P, E])
        BASE = sb("BASE", [P, E])
        TEF = sb("TEF", [P, NS])
        TEI = sb("TEI", [P, NS], I32)
        DST = sb("DST", [P, NT])
        DSTI = sb("DSTI", [P, NT], U32)
        MXP = sb("MXP", [P, 2, HG * TB, 2])
        NMF = sb("NMF", [P, 2, HG * TB])
        NMP = sb("NMP", [P, 2, TB, NPART, HG], BF16)
        NMT = U1[0:NPART * HG, 6656:7168].bitcast(BF16)
        REC = sb("REC", [P, TC, HG])


        PS = ctx.enter_context(nc.psum_tensor("PS", [P, 8, CH], F32))

        x_in = [sem(f"x_in{s}") for s in range(2)]
        w_in, w2_in, w3_in, consts = sem("w_in"), sem("w2_in"), sem("w3_in"), sem("consts")
        fac_bd, wqkv_ps, wqkv_ready = sem("fac_bd"), sem("wqkv_ps"), sem("wqkv_ready")
        var_done, rstd_done = sem("var_done"), sem("rstd_done")
        dve_past, pool_past = sem("dve_past"), sem("pool_past")
        dve_steps, pool_steps = sem("dve_steps"), sem("pool_steps")
        xn_done, z_done, zcopy_done, res_done = (sem(n) for n in ("xn_done", "z_done", "zcopy_done", "res_done"))
        xnT_ps, xnT_ev, qkv_ps, qk_ev, v_ev = (sem(n) for n in ("xnT_ps", "xnT_ev", "qkv_ps", "qk_ev", "v_ev"))
        zT_ps, xfT_ev, lg_ps = (sem(n) for n in ("zT_ps", "xfT_ev", "lg_ps"))
        rest_done, part1_done, parts_done = sem("rest_done"), sem("part1_done"), sem("parts_done")
        parts_out = [sem(f"parts_out{s}") for s in range(2)]
        stack_in = sem("stack_in")
        sh_gu, sh_th, sh_h, sh_y, sh_add = (sem(n) for n in ("sh_gu", "sh_th", "sh_h", "sh_y", "sh_add"))
        mxl_done, tanh_done, score_done, oh_done, rank_ps, place_done = (sem(n) for n in (
            "mxl_done", "tanh_done", "score_done", "oh_done", "rank_ps", "place_done"))
        tile_expert = sem("tile_expert")
        zero_out, scat_out = sem("zero_out"), sem("scat_out")
        xs_in = [sem(f"xs_in{s}") for s in range(2)]
        ys_out = [sem(f"ys_out{s}") for s in range(2)]
        tile_th, tile_h = sem("tile_th"), sem("tile_h")
        yg_in, routed_add = sem("yg_in"), sem("routed_add")
        a_ps, a_max, nm_done, nm_in = (sem(n) for n in ("a_ps", "a_max", "nm_done", "nm_in"))
        misc_ps, misc_read = sem("misc_ps"), sem("misc_read")
        s_ps, p_done, pv_done, o_ev, o_done = (sem(n) for n in ("s_ps", "p_done", "pv_done", "o_ev", "o_done"))
        ones_in, vst_done, out_stored = sem("ones_in"), sem("vst_done"), sem("out_stored")
        block = ctx.enter_context(nc.Block())

        N_W = 12
        N_W2, N_W3 = 3, 2 + IC
        N_STACK = 2 * NSLOT
        FREE = 1
        A_FREE = 2

        def misc(b, ix):
            return ix if b is None else b * len(BAT_IX) + (len(PRE_IX) + ix)

        def tile(b, k):
            return k if b is None else b * NTB + (NPRE + k)

        def tile_pair(b, k):
            return k // 2 if b is None else b * (NTB // 2) + (NPRE + k) // 2

        GATE, UP = slice(0, IC), slice(IC, 2 * IC)

        class Steps:

            def __init__(self, eng, s):
                self.eng, self.sem, self.n, self.off = eng, s, 0, 0

            def done(self, ins):
                self.n += 1
                ins.then_inc(self.sem, 1)
                self.eng.wait_ge(self.sem, self.off + self.n)

            def enter(self, i, k):
                self.off, self.mark, self.k = i * k, self.n, k

            def leave(self, times):
                assert self.n - self.mark == self.k, self.n - self.mark
                self.n, self.off = self.mark + self.k * times, 0

        def quads_of(u):
            return divmod(u + QUADS + LEAD, QUADS)

        @block.sync
        def _(sp):
            for s in parts_out + ys_out + [nm_in]:
                sp.sem_inc(s, FREE)

            def load_x(b, s):
                t = ds(b * (2 * TC) + s * TC, TC)
                sp.dma_start(RES[:, t, :], x_t[:, t, :]).then_inc(x_in[s], 16)

            load_x(0, 0)
            load_x(0, 1)
            for k, (u, v) in enumerate(((UqT, Vq), (UkT, Vk), (UvT, Vv))):
                sp.dma_start(FAC[:, k, 0, :, :], v.rearrange("(g h) r d -> (h r) g d", g=G)).then_inc(w_in, 16)
                sp.dma_start(FAC[:, k, 1, :, :], u.rearrange("(g h) r d -> (h r) g d", g=G)).then_inc(w_in, 16)
            for k, t in enumerate((bq, bk)):
                sp.dma_start(BQK[:, k:k + 1], t.rearrange("h (d o) -> (h d) o", o=1)).then_inc(w_in, 16)
            sp.dma_start(BVR[:, :], bv.rearrange("h d -> (h d)").partition_broadcast(P)).then_inc(w_in, 16)
            for k, t in enumerate((ln_w, ln_b)):
                sp.dma_start(LNC[:, k:k + 1], t.rearrange("(d o) -> d o", o=1)).then_inc(w_in, 16)
            sp.dma_start(RW[:, :], router_w).then_inc(w_in, 16)
            for b in range(1, B):
                for s in range(2):
                    sp.wait_ge(x_in[s], 16 * b)
                    load_x(b, s)
            sp.wait_ge(consts, 1)
            sp.dma_start(slot_x.rearrange("(p a) d -> p a d", p=P),
                         ZER[:, 0:ROW].unsqueeze(1).to_broadcast([P, NS + 2, ROW])).then_inc(zero_out, 16)
            sp.dma_start(KS[KR:KM, :, :, :].rearrange("p a h t -> p (a h t)").rearrange("p (n m) -> p n m", m=P),
                         ONEB[:, :].unsqueeze(1).to_broadcast([NPART, 2 * H * S // P, P])).then_inc(ones_in, 16)

            with sp.Fori(0, B) as b:
                for s in range(2):
                    sp.wait_ge(parts_done, b * 2 + (s + 1 + FREE))
                    for k in range(2):
                        sp.dma_start(split_scr[k, :, :, ds(b * S + s * CH, CH)].rearrange("a p n -> p a n"),
                                     PARTS[:, s, k]).then_inc(parts_out[s], 16)

            def load_stack(b, par):
                for slot in range(NSLOT):
                    rows = slice(slot * DH, (slot + 1) * DH)
                    for k, (T, part) in enumerate(((QS, Q_PART), (KS, K_PART))):
                        src = split_scr[k, part[slot], :, ds(b * S, S)].rearrange("(h d) t -> d h t", h=H)
                        sp.dma_start(T[rows, par, :, :], src).then_inc(stack_in, 16)

            for s in range(2):
                sp.wait_ge(parts_out[s], 16 * 2 * B + FREE)
            load_stack(0, 0)
            sp.dma_start(SHGU[:, 0:I], sh_gate).then_inc(w2_in, 16)
            sp.dma_start(SHGU[:, I:2 * I], sh_up).then_inc(w2_in, 16)
            sp.dma_start(SHD[:, :, :], sh_down.rearrange("(c p) d -> p c d", p=P)).then_inc(w2_in, 16)
            sp.dma_start(WGU[:, :, 0:I], gate_w.rearrange("e d i -> d e i")).then_inc(w3_in, 16)
            sp.dma_start(WGU[:, :, I:2 * I], up_w.rearrange("e d i -> d e i")).then_inc(w3_in, 16)
            for c in range(IC):
                sp.dma_start(WD[:, :, c, :], down_w[:, c * P:(c + 1) * P, :].rearrange("e p d -> p e d")).then_inc(w3_in, 16)
            sp.wait_ge(stack_in, 16 * N_STACK)
            load_stack(1, 1)

            def load_rows(b, k):
                sp.dma_start(XS[:, k % 2, :], slot_x[ds(tile(b, k) * P, P), :]).then_inc(xs_in[k % 2], 16)

            def follow(b, use, ix):
                for kind, k in use.values():
                    if kind == "gu":
                        sp.wait_ge(misc_read, misc(b, ix[kind, k] + 1))
                        load_rows(b, k + 2)
                    if kind == "yx" and (b is not None or k):
                        sp.wait_ge(misc_read, misc(b, ix[kind, k] + 1))
                        sp.dma_start(slot_y[ds(tile(b, k - 1) * P, P), :], YS[:, (k - 1) % 2, :]).then_inc(ys_out[(k - 1) % 2], 16)
                    if kind == "nm":
                        sp.wait_ge(misc_read, misc(b, ix[kind, k] + 1))
                        g, par = k % 2, 0 if b is None else (b + k // 2) % 2
                        for a in range(NPART):
                            sp.dma_start(QS[KR + a:KR + a + 1, par, g * HG:(g + 1) * HG, :],
                                         NMT[a * HG:(a + 1) * HG, :]).then_inc(nm_in, 16)

            sp.wait_ge(scat_out, 16 * NT)
            load_rows(None, 0)
            load_rows(None, 1)
            follow(None, PRE_USE, PRE_IX)
            with sp.Fori(0, B - 2) as b:
                follow(b, BAT_USE, BAT_IX)
                sp.wait_ge(pv_done, b * UPB + (UPB + FREE))
                load_stack(b + 2, b % 2)
            follow(B - 2, BAT_USE, BAT_IX)
            follow(B - 1, END_USE, END_IX)
            sp.wait_ge(routed_add, 2)
            for b in range(B - 1):
                sp.dma_start(out_t[:, b * TB:(b + 1) * TB, :], RES[:, b * TB:(b + 1) * TB, :]).then_inc(out_stored, 16)
            for qh in range(2):
                sp.wait_ge(o_done, (B - 1) * 4 + 3 + qh + FREE)
                t = slice((B - 1) * TB + qh * TC, (B - 1) * TB + (qh + 1) * TC)
                sp.dma_start(out_t[:, t, :], RES[:, t, :]).then_inc(out_stored, 16)
            sp.wait_ge(out_stored, 16 * (B + 1))

        @block.gpsimd
        def _(pool):
            o = Steps(pool, pool_steps)
            for s in (parts_done, res_done, zcopy_done):
                pool.sem_inc(s, FREE)
            nc.gpsimd.memset(ZER[:, :], 0.0)
            nc.gpsimd.memset(ONEB[:, :], 1.0).then_inc(consts, 1)
            nc.gpsimd.memset(IDF[:, :], 0.0)
            nc.gpsimd.memset(NHALF[:, :], -0.5)
            nc.gpsimd.memset(IDB[:, :], 0.0)
            o.done(nc.gpsimd.memset(ONE[:, :], 1.0))
            for m in (IDF, IDB):
                nc.gpsimd.affine_select(out=m[:, :], in_=m[:, :], compare_op=ALU.not_equal, fill=1.0,
                                        base=0, pattern=[[-1, P]], channel_multiplier=1)
            nc.gpsimd.affine_select(out=TRI[:, :], in_=ONE[:, :], compare_op=ALU.is_gt, fill=0.0,
                                    base=0, pattern=[[1, P]], channel_multiplier=-1).then_inc(consts, 1)
            mask = BLK[:, :].rearrange("p (j d) -> p j d", j=HG)
            o.done(nc.gpsimd.affine_select(out=mask, in_=ONE[:, 0:HG * DH].rearrange("p (j d) -> p j d", j=HG),
                                           compare_op=ALU.is_ge, fill=0.0, base=0,
                                           pattern=[[-R, HG], [0, DH]], channel_multiplier=1))
            o.done(nc.gpsimd.affine_select(out=mask, in_=mask, compare_op=ALU.is_ge, fill=0.0, base=R - 1,
                                           pattern=[[R, HG], [0, DH]], channel_multiplier=-1))
            NF = 6 * G
            pool.wait_ge(w_in, 16 * N_W)
            nc.gpsimd.tensor_tensor(FACBD[:, :, :, :, :, :].rearrange("p k f g j d -> p (k f g) j d"),
                                    FAC[:, :].rearrange("p k f g d -> p (k f g) d").unsqueeze(2).to_broadcast([P, NF, HG, DH]),
                                    mask.unsqueeze(1).to_broadcast([P, NF, HG, DH]), ALU.mult).then_inc(fac_bd, 1)
            nc.gpsimd.memset(VALL[:, :, :, DH:DH + 1], 1.0)

            with pool.Fori(0, B) as b:
                for k in range(4):
                    pool.wait_ge(var_done, b * 4 + (k + 1))
                    nc.gpsimd.tensor_tensor(RSTD[:, k % 2, :], RSTD[:, k % 2, :], NHALF[:, :], ALU.pow).then_inc(rstd_done, 1)
                for s in range(2):
                    t = ds(b * TB + s * TC, TC)
                    pool.wait_ge(xn_done, b * 2 + (s + 1))
                    nc.gpsimd.tensor_tensor(RES[:, t, :], RES[:, t, :], XN[:, s], ALU.add).then_inc(res_done, 1)
                for s in range(2):
                    t = ds(b * TB + s * TC, TC)
                    pool.wait_ge(z_done, b * 2 + (s + 1))
                    pool.sem_inc(pool_past, 1)
                    nc.gpsimd.tensor_copy(ZALL[:, t, 0:D], ZS[:, s]).then_inc(zcopy_done, 1)
                for s in range(2):
                    pool.wait_ge(part1_done, b * 2 + (s + 1))
                    nc.gpsimd.tensor_tensor(PARTS[:, s, :, 2, :], QF[:, s], PARTS[:, s, :, 1, :],
                                            ALU.subtract).then_inc(parts_done, 1)

            pool.wait_ge(parts_done, NCH + FREE)
            nc.gpsimd.iota(PREF[:, :, :], pattern=[[0, NT], [-1, E]], base=E, channel_multiplier=0,
                           allow_small_or_imprecise_dtypes=True)
            nc.gpsimd.iota(T128[:, :, :], pattern=[[0, E], [P, NT]], base=0, channel_multiplier=0,
                           allow_small_or_imprecise_dtypes=True)
            nc.gpsimd.iota(TIDX[:, :, :], pattern=[[1, NS], [0, E]], base=0, channel_multiplier=0,
                           allow_small_or_imprecise_dtypes=True).then_inc(consts, 1)

            pool.wait_ge(place_done, 1)
            pool.wait_ge(zero_out, 16)
            for t in range(NT):
                pool.indirect_dma_start(out=slot_x[:, :], out_offset=bass.IndirectOffsetOnAxis(ap=DSTI[:, t:t + 1], axis=0),
                                        in_=ZALL[:, t, :], in_offset=None).then_inc(scat_out, 16)
            for s in range(2):
                pool.wait_ge(parts_out[s], 16 * 2 * B + FREE)
            pool.wait_ge(v_ev, NCH + FREE)
            o.done(nc.gpsimd.memset(U1[:, 4096:6144], 0.0))

            def stage_v(b, g):
                nc.gpsimd.tensor_copy(VST[:, g, :, :, 0:DH + 1],
                                      VALL[:, ds(b * TB, TB), g * HG:(g + 1) * HG, :]).then_inc(vst_done, 1)

            stage_v(0, 0)
            stage_v(0, 1)
            with pool.Fori(0, B - 1) as b:
                for g in range(G):
                    pool.wait_ge(pv_done, b * UPB + ((g + 1) * (UPB // G) + FREE))
                    pool.sem_inc(pool_past, 1)
                    stage_v(b + 1, g)
            for s in range(2):
                pool.wait_ge(ys_out[s], 16 * (NS // 2) + FREE)
            pool.wait_ge(scat_out, 16 * NT)

            def gather(t0, t1):
                for t in range(t0, t1):
                    pool.indirect_dma_start(out=ZALL[:, t, 0:D], out_offset=None, in_=slot_y[:, :],
                                            in_offset=bass.IndirectOffsetOnAxis(ap=DSTI[:, t:t + 1], axis=0)).then_inc(yg_in, 16)

            def add(t0, t1):
                nc.gpsimd.tensor_tensor(RES[:, t0:t1, :], RES[:, t0:t1, :], ZALL[:, t0:t1, 0:D], ALU.add).then_inc(routed_add, 1)

            gather(NT - TB, NT)
            pool.wait_ge(yg_in, 16 * TB)
            pool.wait_ge(sh_add, NCH + FREE)
            add(NT - TB, NT)
            gather(0, NT - TB)
            pool.wait_ge(yg_in, 16 * NT)
            pool.wait_ge(o_done, 4 * (B - 1) + FREE)
            add(0, NT - TB)

        @block.scalar
        def _(act):
            act.wait_ge(consts, 1)
            nc.scalar.activation(REC[:, 0, 0:1], ZER[:, 0:1], ACT.Exp)
            act.sem_inc(qk_ev, FREE)
            act.sem_inc(o_ev, FREE)
            act.wait_ge(w_in, 16 * N_W)
            with act.Fori(0, B) as b:
                for s in range(2):
                    act.wait_ge(xnT_ps, b * 2 + (s + 1 + FREE))
                    nc.scalar.activation(XNT[:, s, :], PS[:, 0, :], ACT.Copy).then_inc(xnT_ev, 1)
                    act.wait_ge(qkv_ps, b * 2 + (s + 1))
                    act.wait_ge(parts_done, b * 2 + FREE)
                    act.wait_ge(parts_out[s], b * 32 + FREE)
                    for k in range(2):
                        nc.scalar.activation(QF[:, s, k, :], PS[:, 2 + k, :], ACT.Identity, bias=BQK[:, k:k + 1])
                        last = nc.scalar.activation(PARTS[:, s, k, 0, :], PS[:, 2 + k, :], ACT.Identity, bias=BQK[:, k:k + 1])
                    last.then_inc(qk_ev, 1)
                for s in range(2):
                    act.wait_ge(rest_done, b * 2 + (s + 1))
                    nc.scalar.activation(PARTS[:, s, :, 1, :], QF[:, s], ACT.Copy).then_inc(part1_done, 1)
                    act.wait_ge(zT_ps, b * 2 + (s + 1 + FREE))
                    act.wait_ge(lg_ps, b * 2 + FREE)
                    affine = dict(bias=LNC[:, 1:2], scale=LNC[:, 0:1])
                    nc.scalar.activation(XTS[:, s, :], PS[:, 1, :], ACT.Identity, **affine)
                    nc.scalar.activation(XFT[:, ds(b * S + s * CH, CH)], PS[:, 1, :], ACT.Identity, **affine).then_inc(xfT_ev, 1)
            act.wait_ge(mxl_done, 1)
            nc.scalar.activation(SCO[:, 0, :], MXL[:, :], ACT.Tanh, scale=0.5).then_inc(tanh_done, 1)
            with act.Fori(0, HG) as h:
                for s in range(2):
                    act.wait_ge(sh_gu, h * 2 + (s + 1))
                    nc.scalar.activation(TH[:, :, :], PS[:, GATE, :], ACT.Tanh, scale=0.5).then_inc(sh_th, 1)

            def read_misc(b, use, ix, gaps):
                for n in gaps:
                    kind, k = use.get(n, (None, None))
                    s = (k or 0) % 2
                    if kind in ("yx", "gu", "ht", "nm"):
                        act.wait_ge(misc_ps, misc(b, ix[kind, k] + 1))
                    if kind == "yx":
                        if b is not None or k:
                            act.wait_ge(ys_out[1 - s], tile_pair(b, k - 1) * 16 + FREE)
                            nc.scalar.activation(YS[:, 1 - s, :], PS[:, 7, 0:D], ACT.Copy)
                        nc.scalar.activation(XET[:, s, :], PS[:, 7, D:D + P], ACT.Identity, bias=LNC[:, 1:2],
                                             scale=LNC[:, 0:1]).then_inc(misc_read, 1)
                    if kind == "gu":
                        nc.scalar.activation(THR[:, s, :], PS[:, 7, 0:I], ACT.Tanh, scale=XS[:, s, D:D + 1]).then_inc(tile_th, 1)
                    if kind == "ht":
                        nc.scalar.activation(HRT[:, s, :], PS[:, 7, 0:I], ACT.Copy).then_inc(misc_read, 1)
                    if kind == "nm":
                        if b is not None:
                            act.wait_ge(nm_in, b * (2 * 16 * NPART) + (k * (16 * NPART) + FREE))
                        nc.scalar.activation(NMT[:, :], PS[0:NPART * HG, 7, :].bitcast(BF16), ACT.Copy).then_inc(misc_read, 1)

            def o_evacuate(b, j):
                act.wait_ge(pv_done, b * UPB + ((j + 1) * TB + FREE))
                act.wait_ge(o_done, b * 4 + (j + FREE))
                nc.scalar.activation(OSB[:, :], PS[:, 6, :], ACT.Copy).then_inc(o_ev, 1)

            def exp(b, u, hp):
                act.wait_ge(s_ps, b * (2 * UPB) + (u * 2 + hp + 1))
                act.wait_ge(pv_done, b * UPB + (max(u - 1, 0) + FREE))
                nc.scalar.activation(PR[:, (u % 2) * 2 + hp], PS[:, 2 * hp:2 * hp + 2, :], ACT.Exp,
                                     scale=SCALE).then_inc(p_done, 1)

            def batch(b, use, ix):
                exp(b, 0, 0)
                exp(b, 0, 1)
                for u in range(UPB):
                    if u % TB == 0 and u:
                        o_evacuate(b, u // TB - 1)
                    if u + 1 < UPB:
                        exp(b, u + 1, 0)
                    read_misc(b, use, ix, (4 * u, 4 * u + 1))
                    if u + 1 < UPB:
                        exp(b, u + 1, 1)
                    read_misc(b, use, ix, (4 * u + 2, 4 * u + 3))
                o_evacuate(b, 2 * G - 1)

            for s in range(2):
                act.wait_ge(parts_out[s], 16 * 2 * B + FREE)
            act.wait_ge(sh_add, NCH + FREE)
            read_misc(None, PRE_USE, PRE_IX, range(PRE_GAPS))
            for b in range(B - 1):
                batch(b, BAT_USE, BAT_IX)
            batch(B - 1, END_USE, END_IX)

        @block.vector
        def _(dve):
            o = Steps(dve, dve_steps)
            dve.sem_inc(a_max, A_FREE)
            for s in (v_ev, sh_h, sh_add, o_done):
                dve.sem_inc(s, FREE)
            o.done(nc.vector.memset(WQKV[:, :, :], 0.0))

            def moments(src, s):
                for j in range(TC):
                    last = nc.vector.bn_stats(ST[:, s, j, :], src(j))
                o.done(last)
                dve.sem_inc(dve_past, 1)
                for j in range(TC):
                    last = nc.vector.bn_aggr(MV[:, s, j, :], ST[:, s, j, :])
                o.done(last)
                nc.vector.tensor_scalar(RSTD[:, s, :], MV[:, s, :, 1], EPS, None, ALU.add).then_inc(var_done, 1)

            def normalize(src, dst, s):
                for j in range(TC):
                    last = nc.vector.tensor_scalar(dst(j), src(j), MV[:, s, j, 0:1], RSTD[:, s, j:j + 1],
                                                   ALU.subtract, ALU.mult)
                return last

            dve.wait_ge(wqkv_ps, 1)
            for g in range(G):
                half = slice(g * HG * DH, (g + 1) * HG * DH)
                last = nc.vector.tensor_copy(WQKV[half, :, half],
                                             PS[half, 0, 0:3 * HG * DH].rearrange("p (k d) -> p k d", k=3))
            last.then_inc(wqkv_ready, 1)
            with dve.Fori(0, B) as b:
                o.enter(b, 8)
                x_tile = lambda s: lambda j: RES[:, b * TB + (s * TC + j), :]
                xn_tile = lambda s: lambda j: XN[:, s, j, :]
                for s in range(2):
                    dve.wait_ge(x_in[s], b * 16 + 16)
                    moments(x_tile(s), s)
                for s in range(2):
                    dve.wait_ge(rstd_done, b * 4 + (s + 1))
                    dve.wait_ge(xnT_ps, b * 2 + FREE)
                    dve.wait_ge(res_done, b * 2 + FREE)
                    normalize(x_tile(s), xn_tile(s), s).then_inc(xn_done, 1)
                    dve.wait_ge(xn_done, b * 2 + (s + 1))
                    moments(xn_tile(s), s)
                for s in range(2):
                    dve.wait_ge(rstd_done, b * 4 + (2 + s + 1))
                    dve.wait_ge(zT_ps, b * 2 + FREE)
                    dve.wait_ge(zcopy_done, b * 2 + FREE)
                    normalize(xn_tile(s), lambda j: ZS[:, s, j, :], s).then_inc(z_done, 1)
                for s in range(2):
                    dve.wait_ge(qk_ev, b * 2 + (s + 1 + FREE))
                    nc.vector.tensor_tensor(QF[:, s], QF[:, s], PARTS[:, s, :, 0, :], ALU.subtract).then_inc(rest_done, 1)
                    dve.wait_ge(qkv_ps, b * 2 + (s + 1))
                    for j in range(TC):
                        last = nc.vector.tensor_tensor(
                            VALL[:, b * TB + (s * TC + j), :, 0:DH],
                            PS[:, 4 + s, j * D:(j + 1) * D].rearrange("p (h d) -> p h d", h=H),
                            BVR[:, :].rearrange("p (h d) -> p h d", h=H), ALU.add)
                    last.then_inc(v_ev, 1)
                o.leave(B)

            per_t = lambda v: v.unsqueeze(2).to_broadcast([P, NT, E])
            dve.wait_ge(lg_ps, NCH + FREE)
            dve.wait_ge(consts, 3)
            o.done(nc.vector.tensor_copy(LG[:, :, :], PS[:, 6, 0:NT * E].rearrange("p (t e) -> p t e", t=NT)))
            nc.vector.tensor_reduce(MXL[:, :], LG[:, :, :], AX.X, ALU.max).then_inc(mxl_done, 1)
            dve.wait_ge(mxl_done, 1)
            o.done(nc.vector.tensor_tensor(OH[:, :, :], LG[:, :, :], per_t(MXL[:, :]), ALU.is_equal))
            o.done(nc.vector.tensor_tensor(OH[:, :, :], OH[:, :, :], PREF[:, :, :], ALU.mult))
            o.done(nc.vector.tensor_reduce(DST[:, :], OH[:, :, :], AX.X, ALU.max))
            nc.vector.tensor_tensor(OH[:, :, :], OH[:, :, :], per_t(DST[:, :]), ALU.is_equal).then_inc(oh_done, 1)
            dve.wait_ge(tanh_done, 1)
            o.done(nc.vector.tensor_scalar(SCO[:, 0, :], SCO[:, 0, :], 0.5, 0.5, ALU.mult, ALU.add))
            nc.vector.tensor_scalar(ZALL[:, :, D], SCO[:, 0, :], 0.5, None, ALU.mult)
            o.done(nc.vector.scalar_tensor_tensor(ZALL[:, :, D + 1], SCO[:, 0, :], 0.5, SCO[:, 0, :], ALU.mult, ALU.mult))
            per_e = lambda v: v.unsqueeze(2).to_broadcast([P, E, NT])
            flat = lambda T: T[:, :, :].rearrange("p a b -> p (a b)")
            dve.wait_ge(rank_ps, 1)
            o.done(nc.vector.tensor_copy(TOT[:, :, :], PS[:, 7, 0:NT * E].rearrange("p (t e) -> p e t", t=NT)))
            o.done(nc.vector.tensor_tensor_scan(flat(INC), flat(TOT), ZER[:, :], 0.0, ALU.add, ALU.add))
            o.done(nc.vector.tensor_tensor(CNT[:, :], INC[:, :, NT - 1], INC[:, :, 0], ALU.subtract))
            o.done(nc.vector.tensor_tensor(CNT[:, :], CNT[:, :], TOT[:, :, 0], ALU.add))
            more = LG[:, :, :].rearrange("p t e -> p (t e)").rearrange("p (e t) -> p e t", e=E)
            o.done(nc.vector.tensor_tensor(more, per_e(CNT[:, :]), T128[:, :, :], ALU.is_gt))
            o.done(nc.vector.tensor_reduce(NTE[:, :], more, AX.X, ALU.add))
            o.done(nc.vector.tensor_tensor_scan(ENDT[:, :], NTE[:, :], ZER[:, 0:E], 0.0, ALU.add, ALU.add))
            o.done(nc.vector.tensor_tensor(NTE[:, :], ENDT[:, :], NTE[:, :], ALU.subtract))
            o.done(nc.vector.tensor_tensor(CNT[:, :], TOT[:, :, 0], INC[:, :, 0], ALU.subtract))
            o.done(nc.vector.scalar_tensor_tensor(BASE[:, :], NTE[:, :], float(P), CNT[:, :], ALU.mult, ALU.add))
            o.done(nc.vector.tensor_tensor(INC[:, :, :], INC[:, :, :], TOT[:, :, :], ALU.subtract))
            o.done(nc.vector.tensor_tensor(INC[:, :, :], INC[:, :, :], per_e(BASE[:, :]), ALU.add))
            o.done(nc.vector.tensor_tensor(LG[:, :, :], PS[:, 6, 0:NT * E].rearrange("p (t e) -> p t e", t=NT),
                                           INC[:, :, :].rearrange("p e t -> p t e"), ALU.add))
            o.done(nc.vector.tensor_tensor(LG[:, :, :], LG[:, :, :], OH[:, :, :], ALU.mult))
            o.done(nc.vector.tensor_reduce(DST[:, :], LG[:, :, :], AX.X, ALU.add))
            nc.vector.tensor_copy(DSTI[:, :], DST[:, :]).then_inc(place_done, 1)
            o.done(nc.vector.tensor_tensor(TIDX[:, :, :], TIDX[:, :, :],
                                           ENDT[:, :].unsqueeze(1).to_broadcast([P, NS, E]), ALU.is_ge))
            o.done(nc.vector.tensor_reduce(TEF[:, :], TIDX[:, :, :], AX.X, ALU.add))
            nc.vector.tensor_scalar(TEI[:, :], TEF[:, :], float(E - 1), None, ALU.min).then_inc(tile_expert, 1)

            def row_max(first, slot, row, j):
                dve.wait_ge(a_ps, first + (j + 1))
                nc.vector.tensor_reduce(MXP[:, slot, row, j % 2:j % 2 + 1], PS[:, 4 + j % 2, :], AX.X, ALU.max).then_inc(a_max, 1)

            dve.wait_ge(res_done, NCH + FREE)
            with dve.Fori(0, HG) as h:
                o.enter(h, 2)

                def hidden(s):
                    dve.wait_ge(sh_th, h * 2 + (s + 1))
                    dve.wait_ge(sh_y, h * 2 + FREE)
                    o.done(nc.vector.scalar_tensor_tensor(HID[:, s, :, :], TH[:, :, :], 1.0, PS[:, GATE, :], ALU.add, ALU.mult))
                    nc.vector.scalar_tensor_tensor(HID[:, s, :, :], HID[:, s, :, :], 0.5, PS[:, UP, :], ALU.mult,
                                                   ALU.mult).then_inc(sh_h, 1)

                def add_shared(s):
                    dve.wait_ge(sh_y, h * 2 + (s + 1 + FREE))
                    t = ds(h * (2 * TC) + s * TC, TC)
                    nc.vector.tensor_tensor(RES[:, t, :], RES[:, t, :], PS[:, 6 + s, :].rearrange("p (t d) -> p t d", t=TC),
                                            ALU.add).then_inc(sh_add, 1)

                def maxima(j0, j1):
                    for j in range(j0, j1):
                        row_max(h * (4 * QUADS // HG), 0, ds(h * TB + j // 2, 1), j)

                maxima(0, 4)
                hidden(0)
                maxima(4, 10)
                hidden(1)
                maxima(10, 12)
                add_shared(0)
                maxima(12, 14)
                add_shared(1)
                maxima(14, 16)
                o.leave(HG)

            def block(b, n):
                ahead, j = divmod(n + 4 * (QUADS + LEAD), 4 * QUADS) if b is not None else (1, n)
                first = (0 if b is None else b * (8 * QUADS)) + ahead * (4 * QUADS)
                row_max(first, ahead % 2, j // 2, j)
                if j == 4 * QUADS - 1:
                    finalize(b * 2 + ahead, ahead % 2, False)

            def finalize(i, slot, first):
                dve.wait_ge(a_max, i * (4 * QUADS) + (4 * QUADS + A_FREE))
                if not first:
                    dve.wait_ge(nm_in, (i - 1) * (16 * NPART) + FREE)
                o.done(nc.vector.tensor_reduce(NMF[:, slot, :], MXP[:, slot, :, :], AX.X, ALU.max, negate=True))
                rest = NMF[:, slot, :].rearrange("p (h t) -> p t h", h=HG)
                for a in range(NPART):
                    part = NMP[:, slot, :, a, :]
                    ins = nc.vector.tensor_copy(part, rest)
                    if a < NPART - 1:
                        o.done(ins)
                        o.done(nc.vector.tensor_tensor(rest, rest, part, ALU.subtract))
                ins.then_inc(nm_done, 1)

            def tile_hidden(b, k):
                s = k % 2
                dve.wait_ge(tile_th, tile(b, k) + 1)
                o.done(nc.vector.scalar_tensor_tensor(HR[:, s, :], THR[:, s, :], 1.0, PS[:, 7, 0:I], ALU.add, ALU.mult))
                nc.vector.scalar_tensor_tensor(HR[:, s, :], HR[:, s, :], XS[:, s, D + 1:D + 2], PS[:, 7, I:2 * I], ALU.mult,
                                               ALU.mult).then_inc(misc_read, 1)

            def output(b, j, ix):
                g, qh = divmod(j, 2)
                dve.wait_ge(misc_ps, misc(b, ix["out", j] + 1))
                o_t = PS[:, 7, :].rearrange("p (t h m) -> p t h m", t=TC, h=HG)
                o.done(nc.vector.reciprocal(REC[:, :, :], o_t[:, :, :, DH]))
                nc.vector.tensor_tensor(OTM[:, :, :, :], o_t[:, :, :, 0:DH],
                                        REC[:, :, :].unsqueeze(3).to_broadcast([P, TC, HG, DH]), ALU.mult).then_inc(misc_read, 1)
                dve.wait_ge(misc_read, misc(b, ix["out", j] + 1))
                dst = RES[:, ds(b * TB + qh * TC, TC), g * HG * DH:(g + 1) * HG * DH]
                nc.vector.tensor_tensor(dst, dst, OTM[:, :, :, :].rearrange("p t h d -> p t (h d)"),
                                        ALU.add).then_inc(o_done, 1)

            def batch(b, last, use, ix, tile_at):
                for n in range(4 * UPB):
                    if not last or n + 4 * (QUADS + LEAD) < 8 * QUADS:
                        block(b, n)
                    kind, k = use.get(n - HID_AFTER, (None, None))
                    if kind == "gu":
                        tile_hidden(b, k)
                    if kind == "out":
                        output(b, k, ix)
                output(b, 2 * G - 1, ix)

            finalize(0, 0, True)
            for n in range(PRE_GAPS):
                if n < 4 * LEAD:
                    block(None, n)
                kind, k = PRE_USE.get(n - HID_AFTER, (None, None))
                if kind == "gu":
                    tile_hidden(None, k)
            for b in range(B - 1):
                batch(b, False, BAT_USE, BAT_IX, TILE_AT)
            dve.wait_ge(routed_add, 1)
            batch(B - 1, True, END_USE, END_IX, ())

        @block.tensor
        def _(pe):
            mm = nc.tensor.matmul
            for s in (xnT_ps, zT_ps, lg_ps, sh_y, pv_done):
                pe.sem_inc(s, FREE)
            pe.wait_ge(fac_bd, 1)
            GD = HG * DH
            for k in range(3):
                for g in range(G):
                    last = mm(PS[g * GD:(g + 1) * GD, 0, k * GD:(k + 1) * GD],
                              FACBD[:, k, 0, g].rearrange("p j d -> p (j d)"),
                              FACBD[:, k, 1, g].rearrange("p j d -> p (j d)"), start=True, stop=True)
            last.then_inc(wqkv_ps, 1)
            pe.wait_ge(consts, 2)
            pe.wait_ge(wqkv_ready, 1)
            with pe.Fori(0, B) as b:
                for s in range(2):
                    pe.wait_ge(xn_done, b * 2 + (s + 1))
                    for j in range(TC):
                        last = nc.tensor.transpose(PS[:, 0, j * P:(j + 1) * P], XN[:, s, j, :], IDF[:, :])
                    last.then_inc(xnT_ps, 1)
                    pe.wait_ge(xnT_ev, b * 2 + (s + 1))
                    pe.wait_ge(qk_ev, b * 2 + (s + FREE))
                    pe.wait_ge(v_ev, b * 2 + FREE)
                    for k in range(2):
                        mm(PS[:, 2 + k, :], WQKV[:, k, :], XNT[:, s, :], start=True, stop=True)
                    for j in range(TC):
                        last = mm(PS[:, 4 + s, j * D:(j + 1) * D], XNT[:, s, j * P:(j + 1) * P], WQKV[:, 2, :],
                                  start=True, stop=True)
                    last.then_inc(qkv_ps, 1)
                for s in range(2):
                    pe.wait_ge(z_done, b * 2 + (s + 1))
                    for j in range(TC):
                        last = nc.tensor.transpose(PS[:, 1, j * P:(j + 1) * P], ZS[:, s, j, :], IDF[:, :])
                    last.then_inc(zT_ps, 1)
                    pe.wait_ge(xfT_ev, b * 2 + (s + 1))
                    for j in range(TC):
                        last = mm(PS[:, 6, ds(b * (TB * E) + (s * TC + j) * E, E)], XTS[:, s, j * P:(j + 1) * P], RW[:, :],
                                  start=True, stop=True)
                    last.then_inc(lg_ps, 1)

            pe.wait_ge(oh_done, 1)
            hot = OH[:, :, :].rearrange("p t e -> p (t e)")
            mm(PS[:, 6, 0:NT * E], TRI[:, :], hot, start=True, stop=True)
            mm(PS[:, 7, 0:NT * E], ONE[:, :], hot, start=True, stop=True).then_inc(rank_ps, 1)

            def block_of_scores(par, head, j, first):
                qt, kh = j // 2 % TB, j % 2
                pe.wait_ge(a_max, first + (j - 1 + A_FREE))
                mm(PS[:, 4 + kh, :], QS[0:KR, par, head, qt * P:(qt + 1) * P],
                   KS[0:KR, par, head, kh * CH:(kh + 1) * CH], start=True, stop=True).then_inc(a_ps, 1)

            pe.wait_ge(w2_in, 16 * N_W2)
            pe.wait_ge(place_done, 1)
            pe.wait_ge(stack_in, 16 * N_STACK)
            with pe.Fori(0, HG) as h:
                def scores_of_head(j0, j1):
                    for j in range(j0, j1):
                        block_of_scores(0, h, j, h * (4 * QUADS // HG))

                def gate_up(s, j0):
                    pe.wait_ge(sh_h, h * 2 + (s + FREE))
                    for j in range(2 * IC):
                        last = mm(PS[:, j, :], SHGU[:, j * P:(j + 1) * P], XFT[:, ds(h * (2 * CH) + s * CH, CH)],
                                  start=True, stop=True)
                        if j == 2 * IC - 1:
                            last.then_inc(sh_gu, 1)
                        scores_of_head(j0 + j, j0 + j + 1)

                def down(s):
                    pe.wait_ge(sh_h, h * 2 + (s + 1 + FREE))
                    pe.wait_ge(sh_add, h * 2 + FREE)
                    for j in range(TC):
                        for i in range(IC):
                            last = mm(PS[:, 6 + s, j * D:(j + 1) * D], HID[:, s, i, j * P:(j + 1) * P], SHD[:, i, :],
                                      start=(i == 0), stop=(i == IC - 1))
                    last.then_inc(sh_y, 1)

                gate_up(0, 0)
                scores_of_head(4, 6)
                gate_up(1, 6)
                down(0)
                scores_of_head(10, 14)
                down(1)
                scores_of_head(14, 16)

            def block(b, n):
                ahead, j = divmod(n + 4 * (QUADS + LEAD), 4 * QUADS) if b is not None else (1, n)
                first = (0 if b is None else b * (8 * QUADS)) + ahead * (4 * QUADS)
                if ahead % 2 == 0 and j == 0:
                    pe.wait_ge(stack_in, b * (16 * N_STACK) + (ahead // 2 + 1) * (16 * N_STACK))
                par = 0 if b is None else (b + ahead // 2) % 2
                block_of_scores(par, ahead % 2 * HG + j // (2 * TB), j, first)

            def expert_of(b, k):
                return pe.value_load(TEI[0:1, ds(tile(b, k), 1)], min_val=0, max_val=E - 1)

            def write_misc(b, use, ix, n):
                if n not in use:
                    return
                kind, k = use[n]
                s = k % 2
                if b is not None or ix[kind, k]:
                    pe.wait_ge(misc_read, misc(b, ix[kind, k]))
                if kind == "yx":
                    if b is not None or k:
                        expert = expert_of(b, k - 1)
                        for i in range(IC):
                            mm(PS[:, 7, 0:D], HRT[:, 1 - s, i * P:(i + 1) * P], WD[:, expert, i, :],
                               start=(i == 0), stop=(i == IC - 1))
                    pe.wait_ge(xs_in[s], tile_pair(b, k) * 16 + 16)
                    last = nc.tensor.transpose(PS[:, 7, D:D + P], XS[:, s, 0:D], IDF[:, :])
                if kind == "gu":
                    last = mm(PS[:, 7, :], XET[:, s, :], WGU[:, expert_of(b, k), :], start=True, stop=True)
                if kind == "ht":
                    for i in range(IC):
                        last = nc.tensor.transpose(PS[:, 7, i * P:(i + 1) * P], HR[:, s, i * P:(i + 1) * P], IDF[:, :])
                if kind == "nm":
                    pe.wait_ge(nm_done, (0 if b is None else b * 2) + (k + 1))
                    rows = PS[0:NPART * HG, 7, :].bitcast(BF16)
                    for t in range(TB):
                        last = nc.tensor.transpose(rows[:, t * P:(t + 1) * P],
                                                   NMP[:, k % 2, t].rearrange("p a h -> p (a h)"), IDB[:, :])
                if kind == "out":
                    pe.wait_ge(o_ev, b * 4 + (k + 1 + FREE))
                    for t in range(TC):
                        last = nc.tensor.transpose(PS[:, 7, t * P:(t + 1) * P], OSB[:, t * P:(t + 1) * P], IDF[:, :])
                last.then_inc(misc_ps, 1)

            def scores(b, u, hp):
                g, qh, kt = u // (2 * TB), u // TB % 2, u % TB
                if qh == 0 and kt == 0 and hp == 0:
                    pe.wait_ge(nm_in, b * (2 * 16 * NPART) + ((g + 1) * (16 * NPART) + FREE))
                if u:
                    pe.wait_ge(p_done, b * (2 * UPB) + (2 * u + hp - 1))
                for j in range(2):
                    head = g * HG + 2 * hp + j
                    last = mm(PS[:, 2 * hp + j, :], KS[0:KM, b % 2, head, kt * P:(kt + 1) * P],
                              QS[0:KM, b % 2, head, qh * CH:(qh + 1) * CH], start=True, stop=True)
                last.then_inc(s_ps, 1)

            def values(b, u, part):
                g, qh, kt = u // (2 * TB), u // TB % 2, u % TB
                q = slice(part * (CH // 2), (part + 1) * (CH // 2))
                if part == 0:
                    if kt == 0:
                        pe.wait_ge(o_ev, b * 4 + (u // TB + FREE))
                    if kt == 0 and qh == 0:
                        pe.wait_ge(vst_done, b * G + (g + 1))
                    pe.wait_ge(p_done, b * (2 * UPB) + (2 * u + 2))
                for j in range(HG):
                    last = mm(PS[j * VM:(j + 1) * VM, 6, q], VST[:, g, kt, j, :], PR[:, (u % 2) * 2 + j // 2, j % 2, q],
                              start=(kt == 0 and part == 0), stop=(kt == TB - 1 and part == 1))
                if part == 1:
                    last.then_inc(pv_done, 1)

            def batch(b, last, use, ix):
                scores(b, 0, 0)
                scores(b, 0, 1)
                for u in range(UPB):
                    for gap in range(4):
                        if gap < 2 and u + 1 < UPB:
                            scores(b, u + 1, gap)
                        if gap >= 2:
                            values(b, u, gap - 2)
                        n = 4 * u + gap
                        if not last or n + 4 * (QUADS + LEAD) < 8 * QUADS:
                            block(b, n)
                        write_misc(b, use, ix, n)
                write_misc(b, use, ix, OUT_AT[-1])

            pe.wait_ge(ones_in, 16)
            pe.wait_ge(sh_add, NCH + FREE)
            pe.wait_ge(tile_expert, 1)
            pe.wait_ge(w3_in, 16 * N_W3)
            for n in range(PRE_GAPS):
                if n < 4 * LEAD:
                    block(None, n)
                write_misc(None, PRE_USE, PRE_IX, n)
            for b in range(B - 1):
                batch(b, False, BAT_USE, BAT_IX)
            batch(B - 1, True, END_USE, END_IX)


_INS = ["x", "Uq", "Vq", "bq", "Uk", "Vk", "bk", "Uv", "Vv", "bv", "ln_w", "ln_b", "router_w",
        "gate_w", "up_w", "down_w", "sh_gate", "sh_up", "sh_down"]


def kernel(**inputs):
    import numpy as _np
    import concourse.bacc as _bacc
    from concourse import mybir as _mybir
    from concourse.bass_utils import run_bass_kernel_spmd as _run

    nc = _bacc.Bacc("TRN2", target_bir_lowering=False, num_devices=1)
    arrays, args = {}, []
    for name in _INS:
        full = next(k for k in inputs if k in (f"L0_attn_{name}", f"L0_ffn_{name}"))
        a = _np.asarray(inputs[full])
        if name in ("Uq", "Uk", "Uv"):
            a = a.transpose(0, 2, 1)
        a = _np.ascontiguousarray(a)
        arrays[f"in_{name}_dram"] = a
        args.append(nc.dram_tensor(f"in_{name}_dram", a.shape, _mybir.dt.from_np(a.dtype), kind="ExternalInput").ap())
    dt = _mybir.dt.from_np(_np.dtype("float32"))
    args.append(nc.dram_tensor("out_0_dram", (4, 1024, 128), dt, kind="ExternalOutput").ap())
    build_kernel(nc, *args)
    r = _run(nc, [arrays], core_ids=[0])
    return r.results[0]["out_0_dram"]
```

```python
import concourse.bass as bass
from concourse import mybir
from contextlib import ExitStack


def build_kernel(nc, x, UqT, Vq, bq, UkT, Vk, bk, UvT, Vv, bv, ln_w, ln_b, router_w,
                 gate_w, up_w, down_w, sh_gate, sh_up, sh_down, out):
    F32, BF16 = mybir.dt.float32, mybir.dt.bfloat16
    I32, U32 = mybir.dt.int32, mybir.dt.uint32
    ALU, ACT, AX = mybir.AluOpType, mybir.ActivationFunctionType, mybir.AxisListType
    ds = bass.ds
    nc.disable_value_cache = True

    P = 128
    B, S, D = x.shape
    H, R, DH = Vq.shape
    E, _, I = gate_w.shape
    NT, TB = B * S // P, S // P
    CH = 512
    TC = CH // P
    NCH = B * S // CH
    HG = 4
    G = H // HG
    IC = I // P
    NS = -(-(B * S + E * (P - 1)) // P)
    EPS, SCALE = 1e-5, float(DH) ** -0.5
    Q_PART = (0, 0, 0, 1, 1, 2)
    K_PART = (0, 1, 2, 0, 1, 0)
    NPART, NSLOT = 3, len(Q_PART)
    KR = NSLOT * DH
    KM = KR + NPART
    VM = 32
    UPB = G * 2 * TB
    QUADS = HG * TB * 2 // 4
    LEAD = 4
    ROW = D + 2

    TILE_AT = (6, 14, 22, 30, 42, 54, 62, 74, 82, 90, 102, 110, 122)
    STAGES = {"yx": 0, "gu": 2, "ht": 5}
    HID_AFTER = 1
    OUT_AT = (3, 39, 71, 99)
    NM_AT = {4 * (QUADS - LEAD) + 3: 1, 4 * (2 * QUADS - LEAD) + 5: 2}
    GAP_BLOCKS, ROUTE_BLOCKS = (2, 3, 2, 2), 12
    PRE_AT, PRE_STAGES, PRE_NM = (19, 23), {"yx": 0, "gu": 1, "ht": 3}, {28: 0}
    NPRE, NTB = len(PRE_AT), len(TILE_AT)
    NBT = -(-(NS - NPRE) // NTB)
    NS = NPRE + NBT * NTB
    assert NBT == B - 1

    def uses(tile_at, stages, nm_at, out_at):
        found = [(n + d, kind, k) for k, n in enumerate(tile_at) for kind, d in stages.items()]
        found += [(n, "nm", a) for n, a in nm_at.items()] + [(n, "out", j) for n, j in out_at.items()]
        found.sort()
        assert len({n for n, _, _ in found}) == len(found)
        return {n: (kind, k) for n, kind, k in found}, {(kind, k): i for i, (_, kind, k) in enumerate(found)}

    NJ = 2 * G
    PRE_USE, PRE_IX = uses(PRE_AT, PRE_STAGES, PRE_NM, {})
    USE, IX, BEFORE = [], [], [len(PRE_IX)]
    for b in range(B):
        last = b == B - 1
        outs = {n: b * NJ + j - 1 for j, n in enumerate(OUT_AT) if b * NJ + j}
        if last:
            outs[4 * UPB] = B * NJ - 1
        use, ix = uses(TILE_AT[:1] if last else TILE_AT, {"yx": 0} if last else STAGES,
                       {n: a for n, a in NM_AT.items() if not (last and a == 2)}, outs)
        USE.append(use), IX.append(ix), BEFORE.append(BEFORE[-1] + len(ix))

    split_scr = nc.dram_tensor("split_scr", [2, NPART, D, B * S], BF16, kind="Internal").ap()
    slot_x = nc.dram_tensor("slot_x", [(NS + 2) * P, ROW], F32, kind="Internal").ap()
    slot_y = nc.dram_tensor("slot_y", [NS * P, D], F32, kind="Internal").ap()
    x_t = x.rearrange("b (t p) d -> p (b t) d", p=P)
    out_t = out.rearrange("b (t p) d -> p (b t) d", p=P)

    ctx = ExitStack()
    with ctx:
        def sb(name, shape, dt=F32):
            return ctx.enter_context(nc.sbuf_tensor(name, shape, dt))

        def sem(name):
            return ctx.enter_context(nc.semaphore(name))

        QS = sb("QS", [P, 2, H, S], BF16)
        KS = sb("KS", [P, 2, H, S], BF16)
        VALL = sb("VALL", [P, NT, H, DH + 1])
        RES = sb("RES", [P, NT, D])
        ZALL = sb("ZALL", [P, NT, ROW])
        XFT = sb("XFT", [P, B * S])
        U1 = sb("U1", [P, 7168])
        XN = U1[:, 0:1024].rearrange("p (s t d) -> p s t d", s=2, t=TC)
        XNT = U1[:, 1024:2048].rearrange("p (s n) -> p s n", s=2)
        QF = U1[:, 2048:4096].rearrange("p (s k n) -> p s k n", s=2, k=2)
        PARTS = U1[:, 4096:7168].bitcast(BF16).rearrange("p (s k a n) -> p s k a n", s=2, k=2, a=NPART)
        TH = U1[:, 0:1024].rearrange("p (c n) -> p c n", c=IC)
        HID = U1[:, 1024:3072].rearrange("p (s c n) -> p s c n", s=2, c=IC)
        PREF = U1[:, 2048:2304].rearrange("p (t e) -> p t e", t=NT)
        T128 = U1[:, 2304:2560].rearrange("p (e t) -> p e t", e=E)
        TIDX = U1[:, 2560:2560 + NS * E].rearrange("p (t e) -> p t e", t=NS)
        TOT = U1[:, 3072:3328].rearrange("p (e t) -> p e t", e=E)
        INC = U1[:, 3328:3584].rearrange("p (e t) -> p e t", e=E)
        PR = U1[:, 0:4096].rearrange("p (s j n) -> p s j n", s=4, j=2)
        VST = U1[:, 4096:6144].rearrange("p (g t j m) -> p g t j m", g=G, t=TB, j=HG)
        OSB = U1[:, 6144:6656]
        U2 = sb("U2", [P, 2308 + 256])
        FACBD = U2[:, 0:6 * G * HG * DH].rearrange(
            "p (k f g j d) -> p k f g j d", k=3, f=2, g=G, j=HG)
        THR = U2[:, 0:512].rearrange("p (s n) -> p s n", s=2)
        HR = U2[:, 512:1024].rearrange("p (s n) -> p s n", s=2)
        HRT = U2[:, 1024:1536].rearrange("p (s n) -> p s n", s=2)
        XS = U2[:, 2304:2304 + 2 * ROW].rearrange("p (s n) -> p s n", s=2)
        XET = U2[:, 1792:2048].rearrange("p (s n) -> p s n", s=2)
        OTM = U2[:, 1536:1792].rearrange("p (t h d) -> p t h d", t=TC, h=HG)
        YS = U2[:, 2048:2304].rearrange("p (s n) -> p s n", s=2)
        WGU = sb("WGU", [P, E, 2 * I])
        WD = sb("WD", [P, E, IC, D])
        SHGU = sb("SHGU", [P, 2 * I])
        SHD = sb("SHD", [P, IC, D])
        RW = sb("RW", [P, E])
        FAC = sb("FAC", [P, 3, 2, G, DH])
        BLK = sb("BLK", [P, HG * DH])
        WQKV = sb("WQKV", [P, 3, D])
        BQK = sb("BQK", [P, 2])
        LNC = sb("LNC", [P, 2])
        BVR = sb("BVR", [P, D])
        IDF = sb("IDF", [P, P])
        IDB = sb("IDB", [P, P], BF16)
        TRI = sb("TRI", [P, P])
        ONE = sb("ONE", [P, P])
        ONEB = sb("ONEB", [NPART, P], BF16)
        ST = sb("ST", [P, 4, TC, 6])
        MV = sb("MV", [P, 4, TC, 2])
        RSTD = sb("RSTD", [P, 4, TC])
        NHALF = sb("NHALF", [P, TC])
        LG = sb("LG", [P, NT, E])
        MXL = sb("MXL", [P, NT])
        OH = sb("OH", [P, NT, E])
        SCO = sb("SCO", [P, 2, NT])
        ZER = sb("ZER", [P, E * NT])
        CNT = sb("CNT", [P, E])
        NTE = sb("NTE", [P, E])
        ENDT = sb("ENDT", [P, E])
        BASE = sb("BASE", [P, E])
        TEF = sb("TEF", [P, NS])
        TEI = sb("TEI", [P, NS], I32)
        DST = sb("DST", [P, NT])
        DSTI = sb("DSTI", [P, NT], U32)
        MXP = sb("MXP", [P, 2, HG * TB, 2])
        NMF = sb("NMF", [P, 2, HG * TB])
        NMP = sb("NMP", [P, 2, TB, NPART, HG], BF16)
        NMT = U1[0:NPART * HG, 6656:7168].bitcast(BF16)
        REC = sb("REC", [P, TC, HG])


        PS = ctx.enter_context(nc.psum_tensor("PS", [P, 8, CH], F32))

        x_in = [sem(f"x_in{s}") for s in range(2)]
        w_in, w2_in, w3_in, consts = sem("w_in"), sem("w2_in"), sem("w3_in"), sem("consts")
        fac_bd, wqkv_ps, wqkv_ready = sem("fac_bd"), sem("wqkv_ps"), sem("wqkv_ready")
        var_done, rstd_done = sem("var_done"), sem("rstd_done")
        pool_past = sem("pool_past")
        dve_steps, pool_steps = sem("dve_steps"), sem("pool_steps")
        xn_done, z_done, res_done = (sem(n) for n in ("xn_done", "z_done", "res_done"))
        xnT_ps, xnT_ev, qkv_ps, qk_ev, v_ev = (sem(n) for n in ("xnT_ps", "xnT_ev", "qkv_ps", "qk_ev", "v_ev"))
        zT_ps, xfT_ev, lg_ps = (sem(n) for n in ("zT_ps", "xfT_ev", "lg_ps"))
        rest_done, part1_done, parts_done = sem("rest_done"), sem("part1_done"), sem("parts_done")
        parts_out = [sem(f"parts_out{s}") for s in range(2)]
        stack_in = sem("stack_in")
        sh_gu, sh_th, sh_h, sh_y, sh_add = (sem(n) for n in ("sh_gu", "sh_th", "sh_h", "sh_y", "sh_add"))
        mxl_done, tanh_done, score_done, oh_done, rank_ps, place_done = (sem(n) for n in (
            "mxl_done", "tanh_done", "score_done", "oh_done", "rank_ps", "place_done"))
        tile_expert = sem("tile_expert")
        zero_out, scat_out = sem("zero_out"), sem("scat_out")
        xs_in = [sem(f"xs_in{s}") for s in range(2)]
        ys_out = [sem(f"ys_out{s}") for s in range(2)]
        tile_th, tile_h = sem("tile_th"), sem("tile_h")
        yg_in, routed_add = sem("yg_in"), sem("routed_add")
        a_ps, a_max, nm_done, nm_in = (sem(n) for n in ("a_ps", "a_max", "nm_done", "nm_in"))
        misc_ps, misc_read = sem("misc_ps"), sem("misc_read")
        s_ps, p_done, pv_done, o_ev, o_done = (sem(n) for n in ("s_ps", "p_done", "pv_done", "o_ev", "o_done"))
        ones_in, vst_done, out_stored = sem("ones_in"), sem("vst_done"), sem("out_stored")
        block = ctx.enter_context(nc.Block())

        N_W = 12
        N_W2, N_W3 = 3, 2 + IC
        N_STACK = 2 * NSLOT
        SHARES = 3

        def misc(b, ix):
            return ix if b is None else BEFORE[b] + ix

        def tile(b, k):
            return k if b is None else b * NTB + (NPRE + k)

        def pre_blocks(n):
            c, gap = divmod(n, 4)
            first = ROUTE_BLOCKS + c * sum(GAP_BLOCKS) + sum(GAP_BLOCKS[:gap])
            return range(first, min(first + GAP_BLOCKS[gap], 4 * (QUADS + LEAD)))

        class Steps:

            def __init__(self, eng, s):
                self.eng, self.sem, self.n = eng, s, 0

            def done(self, ins):
                self.n += 1
                ins.then_inc(self.sem, 1)
                self.eng.wait_ge(self.sem, self.n)

        @block.sync
        def _(sp):
            def load_x(b, s):
                t = ds(b * (2 * TC) + s * TC, TC)
                sp.dma_start(RES[:, t, :], x_t[:, t, :]).then_inc(x_in[s], 16)

            load_x(0, 0)
            load_x(0, 1)
            for k, (u, v) in enumerate(((UqT, Vq), (UkT, Vk), (UvT, Vv))):
                sp.dma_start(FAC[:, k, 0, :, :], v.rearrange("(g h) r d -> (h r) g d", g=G)).then_inc(w_in, 16)
                sp.dma_start(FAC[:, k, 1, :, :], u.rearrange("(g h) r d -> (h r) g d", g=G)).then_inc(w_in, 16)
            for k, t in enumerate((bq, bk)):
                sp.dma_start(BQK[:, k:k + 1], t.rearrange("h (d o) -> (h d) o", o=1)).then_inc(w_in, 16)
            sp.dma_start(BVR[:, :], bv.rearrange("h d -> (h d)").partition_broadcast(P)).then_inc(w_in, 16)
            for k, t in enumerate((ln_w, ln_b)):
                sp.dma_start(LNC[:, k:k + 1], t.rearrange("(d o) -> d o", o=1)).then_inc(w_in, 16)
            sp.dma_start(RW[:, :], router_w).then_inc(w_in, 16)
            for b in range(1, B):
                for s in range(2):
                    sp.wait_ge(x_in[s], 16 * b)
                    load_x(b, s)
            sp.wait_ge(consts, 1)
            sp.dma_start(slot_x.rearrange("(p a) d -> p a d", p=P),
                         ZER[:, 0:ROW].unsqueeze(1).to_broadcast([P, NS + 2, ROW])).then_inc(zero_out, 16)
            sp.dma_start(KS[KR:KM, :, :, :].rearrange("p a h t -> p (a h t)").rearrange("p (n m) -> p n m", m=P),
                         ONEB[:, :].unsqueeze(1).to_broadcast([NPART, 2 * H * S // P, P])).then_inc(ones_in, 16)

            def load_stack(b, part, parts=1):
                par = b % 2
                for slot in range(part * NSLOT // parts, (part + 1) * NSLOT // parts):
                    rows = slice(slot * DH, (slot + 1) * DH)
                    for k, (T, which) in enumerate(((QS, Q_PART), (KS, K_PART))):
                        src = split_scr[k, which[slot], :, b * S:(b + 1) * S].rearrange("(h d) t -> d h t", h=H)
                        sp.dma_start(T[rows, par, :, :], src).then_inc(stack_in, 16)

            for c in range(NCH):
                if c == 2:
                    for s in range(2):
                        sp.wait_ge(parts_out[s], 32)
                sp.wait_ge(parts_done, c + 1)
                for k in range(2):
                    sp.dma_start(split_scr[k, :, :, c * CH:(c + 1) * CH].rearrange("a p n -> p a n"),
                                 PARTS[:, c % 2, k]).then_inc(parts_out[c % 2], 16)
                if c == 1:
                    sp.dma_start(SHGU[:, 0:I], sh_gate).then_inc(w2_in, 16)
                    sp.dma_start(SHGU[:, I:2 * I], sh_up).then_inc(w2_in, 16)
                    sp.dma_start(SHD[:, :, :], sh_down.rearrange("(c p) d -> p c d", p=P)).then_inc(w2_in, 16)
                if 2 <= c < 2 + SHARES:
                    load_stack(0, c - 2, SHARES)
            sp.dma_start(WGU[:, :, 0:I], gate_w.rearrange("e d i -> d e i")).then_inc(w3_in, 16)
            sp.dma_start(WGU[:, :, I:2 * I], up_w.rearrange("e d i -> d e i")).then_inc(w3_in, 16)
            for c in range(IC):
                sp.dma_start(WD[:, :, c, :], down_w[:, c * P:(c + 1) * P, :].rearrange("e p d -> p e d")).then_inc(w3_in, 16)
            for s in range(2):
                sp.wait_ge(parts_out[s], 16 * 2 * B)
            sp.wait_ge(stack_in, 16 * N_STACK)
            load_stack(1, 0)

            def load_rows(b, k):
                sp.dma_start(XS[:, tile(b, k) % 2, :], slot_x[ds(tile(b, k) * P, P), :]).then_inc(xs_in[tile(b, k) % 2], 16)

            def follow(b, use, ix):
                for kind, k in use.values():
                    if kind == "gu":
                        sp.wait_ge(misc_read, misc(b, ix[kind, k] + 1))
                        load_rows(b, k + 2)
                    if kind == "yx" and (b is not None or k):
                        sp.wait_ge(misc_read, misc(b, ix[kind, k] + 1))
                        t = tile(b, k) - 1
                        sp.dma_start(slot_y[t * P:(t + 1) * P, :], YS[:, t % 2, :]).then_inc(ys_out[t % 2], 16)
                    if kind == "nm":
                        sp.wait_ge(misc_read, misc(b, ix[kind, k] + 1))
                        g, par = k % 2, 0 if b is None else (b + k // 2) % 2
                        for a in range(NPART):
                            sp.dma_start(QS[KR + a:KR + a + 1, par, g * HG:(g + 1) * HG, :],
                                         NMT[a * HG:(a + 1) * HG, :]).then_inc(nm_in, 16)

            sp.wait_ge(scat_out, 16 * NT)
            load_rows(None, 0)
            load_rows(None, 1)
            follow(None, PRE_USE, PRE_IX)
            for b in range(B - 1):
                follow(b, USE[b], IX[b])
                if b + 2 < B:
                    sp.wait_ge(pv_done, (b + 1) * UPB)
                    load_stack(b + 2, 0)
            follow(B - 1, USE[B - 1], IX[B - 1])
            sp.wait_ge(routed_add, 2)
            for b in range(B - 1):
                sp.dma_start(out_t[:, b * TB:(b + 1) * TB, :], RES[:, b * TB:(b + 1) * TB, :]).then_inc(out_stored, 16)
            for qh in range(2):
                sp.wait_ge(o_done, (B - 1) * 4 + 3 + qh)
                t = slice((B - 1) * TB + qh * TC, (B - 1) * TB + (qh + 1) * TC)
                sp.dma_start(out_t[:, t, :], RES[:, t, :]).then_inc(out_stored, 16)
            sp.wait_ge(out_stored, 16 * (B + 1))

        @block.gpsimd
        def _(pool):
            o = Steps(pool, pool_steps)
            nc.gpsimd.memset(ZER[:, :], 0.0)
            nc.gpsimd.memset(ONEB[:, :], 1.0).then_inc(consts, 1)
            nc.gpsimd.memset(IDF[:, :], 0.0)
            nc.gpsimd.memset(NHALF[:, :], -0.5)
            nc.gpsimd.memset(IDB[:, :], 0.0)
            o.done(nc.gpsimd.memset(ONE[:, :], 1.0))
            for m in (IDF, IDB):
                nc.gpsimd.affine_select(out=m[:, :], in_=m[:, :], compare_op=ALU.not_equal, fill=1.0,
                                        base=0, pattern=[[-1, P]], channel_multiplier=1)
            nc.gpsimd.affine_select(out=TRI[:, :], in_=ONE[:, :], compare_op=ALU.is_gt, fill=0.0,
                                    base=0, pattern=[[1, P]], channel_multiplier=-1).then_inc(consts, 1)
            mask = BLK[:, :].rearrange("p (j d) -> p j d", j=HG)
            o.done(nc.gpsimd.affine_select(out=mask, in_=ONE[:, 0:HG * DH].rearrange("p (j d) -> p j d", j=HG),
                                           compare_op=ALU.is_ge, fill=0.0, base=0,
                                           pattern=[[-R, HG], [0, DH]], channel_multiplier=1))
            o.done(nc.gpsimd.affine_select(out=mask, in_=mask, compare_op=ALU.is_ge, fill=0.0, base=R - 1,
                                           pattern=[[R, HG], [0, DH]], channel_multiplier=-1))
            nc.gpsimd.memset(VALL[:, :, :, DH:DH + 1], 1.0)

            def root(v, slot):
                pool.wait_ge(var_done, v + 1)
                nc.gpsimd.tensor_tensor(RSTD[:, slot, :], RSTD[:, slot, :], NHALF[:, :], ALU.pow).then_inc(rstd_done, 1)

            def block_diagonal_factors():
                NF = 6 * G
                pool.wait_ge(w_in, 16 * N_W)
                nc.gpsimd.tensor_tensor(FACBD[:, :, :, :, :, :].rearrange("p k f g j d -> p (k f g) j d"),
                                        FAC[:, :].rearrange("p k f g d -> p (k f g) d").unsqueeze(2).to_broadcast([P, NF, HG, DH]),
                                        mask.unsqueeze(1).to_broadcast([P, NF, HG, DH]), ALU.mult).then_inc(fac_bd, 1)

            root(0, 0)
            for n in range(NCH + 2):
                if n + 1 < NCH:
                    root(2 * n + 1, (n + 1) % 2)
                if n == 0:
                    block_diagonal_factors()
                if n < NCH:
                    root(2 * n + (2 if n + 1 < NCH else 1), 2 + n % 2)
                    t = slice(n * TC, (n + 1) * TC)
                    pool.wait_ge(xn_done, n + 1)
                    nc.gpsimd.tensor_tensor(RES[:, t, :], RES[:, t, :], XN[:, n % 2], ALU.add).then_inc(res_done, 1)
                if n >= 2:
                    s = n % 2
                    pool.wait_ge(part1_done, n - 1)
                    nc.gpsimd.tensor_tensor(PARTS[:, s, :, 2, :], QF[:, s], PARTS[:, s, :, 1, :],
                                            ALU.subtract).then_inc(parts_done, 1)

            pool.wait_ge(parts_done, NCH)
            nc.gpsimd.iota(PREF[:, :, :], pattern=[[0, NT], [-1, E]], base=E, channel_multiplier=0,
                           allow_small_or_imprecise_dtypes=True)
            nc.gpsimd.iota(T128[:, :, :], pattern=[[0, E], [P, NT]], base=0, channel_multiplier=0,
                           allow_small_or_imprecise_dtypes=True)
            nc.gpsimd.iota(TIDX[:, :, :], pattern=[[1, NS], [0, E]], base=0, channel_multiplier=0,
                           allow_small_or_imprecise_dtypes=True).then_inc(consts, 1)

            pool.wait_ge(place_done, 1)
            pool.wait_ge(zero_out, 16)
            for t in range(NT):
                pool.indirect_dma_start(out=slot_x[:, :], out_offset=bass.IndirectOffsetOnAxis(ap=DSTI[:, t:t + 1], axis=0),
                                        in_=ZALL[:, t, :], in_offset=None).then_inc(scat_out, 16)
            for s in range(2):
                pool.wait_ge(parts_out[s], 16 * 2 * B)
            pool.wait_ge(v_ev, NCH)
            o.done(nc.gpsimd.memset(U1[:, 4096:6144], 0.0))

            def stage_v(b, g):
                nc.gpsimd.tensor_copy(VST[:, g, :, :, 0:DH + 1],
                                      VALL[:, ds(b * TB, TB), g * HG:(g + 1) * HG, :]).then_inc(vst_done, 1)

            stage_v(0, 0)
            stage_v(0, 1)
            with pool.Fori(0, B - 1) as b:
                for g in range(G):
                    pool.wait_ge(pv_done, b * UPB + ((g + 1) * (UPB // G)))
                    pool.sem_inc(pool_past, 1)
                    stage_v(b + 1, g)
            for s in range(2):
                pool.wait_ge(ys_out[s], 16 * ((NS + 1 - s) // 2))
            pool.wait_ge(scat_out, 16 * NT)

            def gather(t0, t1):
                for t in range(t0, t1):
                    pool.indirect_dma_start(out=ZALL[:, t, 0:D], out_offset=None, in_=slot_y[:, :],
                                            in_offset=bass.IndirectOffsetOnAxis(ap=DSTI[:, t:t + 1], axis=0)).then_inc(yg_in, 16)

            def add(t0, t1):
                nc.gpsimd.tensor_tensor(RES[:, t0:t1, :], RES[:, t0:t1, :], ZALL[:, t0:t1, 0:D], ALU.add).then_inc(routed_add, 1)

            gather(NT - TB, NT)
            pool.wait_ge(yg_in, 16 * TB)
            pool.wait_ge(sh_add, NCH)
            add(NT - TB, NT)
            gather(0, NT - TB)
            pool.wait_ge(yg_in, 16 * NT)
            pool.wait_ge(o_done, 4 * (B - 1))
            add(0, NT - TB)

        @block.scalar
        def _(act):
            act.wait_ge(consts, 1)
            nc.scalar.activation(REC[:, 0, 0:1], ZER[:, 0:1], ACT.Exp)
            for n in range(NCH + 2):
                s, z = n % 2, (n - 1) % 2
                if n < NCH:
                    act.wait_ge(xnT_ps, n + 1)
                    if n >= 2:
                        act.wait_ge(qkv_ps, n - 1)
                    nc.scalar.activation(XNT[:, s, :], PS[:, 0, :], ACT.Copy).then_inc(xnT_ev, 1)
                if n >= 2:
                    act.wait_ge(rest_done, n - 1)
                    nc.scalar.activation(PARTS[:, s, :, 1, :], QF[:, s], ACT.Copy).then_inc(part1_done, 1)
                if 1 <= n <= NCH:
                    act.wait_ge(qkv_ps, n)
                    if n == 1:
                        act.wait_ge(w_in, 16 * N_W)
                    if n >= 3:
                        act.wait_ge(parts_done, n - 2)
                        act.wait_ge(parts_out[z], 32 * ((n - 1) // 2))
                    for k in range(2):
                        nc.scalar.activation(QF[:, z, k, :], PS[:, 2 + k, :], ACT.Identity, bias=BQK[:, k:k + 1])
                        last = nc.scalar.activation(PARTS[:, z, k, 0, :], PS[:, 2 + k, :], ACT.Identity, bias=BQK[:, k:k + 1])
                    last.then_inc(qk_ev, 1)
                    act.wait_ge(zT_ps, n)
                    nc.scalar.activation(XFT[:, (n - 1) * CH:n * CH], PS[:, 1, :], ACT.Identity, bias=LNC[:, 1:2],
                                         scale=LNC[:, 0:1]).then_inc(xfT_ev, 1)
            act.wait_ge(mxl_done, 1)
            nc.scalar.activation(SCO[:, 0, :], MXL[:, :], ACT.Tanh, scale=0.5).then_inc(tanh_done, 1)
            def read_misc(b, use, ix, gaps):
                for n in gaps:
                    kind, k = use.get(n, (None, None))
                    s = tile(b, k or 0) % 2
                    if kind in ("yx", "gu", "ht", "nm"):
                        act.wait_ge(misc_ps, misc(b, ix[kind, k] + 1))
                    if kind == "yx":
                        if b is not None or k:
                            if tile(b, k) >= 3:
                                act.wait_ge(ys_out[1 - s], (tile(b, k) - 1) // 2 * 16)
                            nc.scalar.activation(YS[:, 1 - s, :], PS[:, 7, 0:D], ACT.Copy)
                        nc.scalar.activation(XET[:, s, :], PS[:, 7, D:D + P], ACT.Identity, bias=LNC[:, 1:2],
                                             scale=LNC[:, 0:1]).then_inc(misc_read, 1)
                    if kind == "gu":
                        nc.scalar.activation(THR[:, s, :], PS[:, 7, 0:I], ACT.Tanh, scale=XS[:, s, D:D + 1]).then_inc(tile_th, 1)
                    if kind == "ht":
                        nc.scalar.activation(HRT[:, s, :], PS[:, 7, 0:I], ACT.Copy).then_inc(misc_read, 1)
                    if kind == "nm":
                        if b is not None:
                            act.wait_ge(nm_in, b * (2 * 16 * NPART) + (k * (16 * NPART)))
                        nc.scalar.activation(NMT[:, :], PS[0:NPART * HG, 7, :].bitcast(BF16), ACT.Copy).then_inc(misc_read, 1)

            def o_evacuate(j):
                act.wait_ge(pv_done, (j + 1) * TB)
                if j:
                    act.wait_ge(o_done, j)
                nc.scalar.activation(OSB[:, :], PS[:, 6, :], ACT.Copy).then_inc(o_ev, 1)

            def exp(v, hp):
                if v == B * UPB:
                    return
                act.wait_ge(s_ps, v * 2 + hp + 1)
                if v >= 2:
                    act.wait_ge(pv_done, v - 1)
                nc.scalar.activation(PR[:, (v % 2) * 2 + hp], PS[:, 2 * hp:2 * hp + 2, :], ACT.Exp,
                                     scale=SCALE).then_inc(p_done, 1)

            def batch(b, use, ix):
                for u in range(UPB):
                    v = b * UPB + u
                    if v == 0:
                        act.wait_ge(sh_y, NCH)
                    if v and v % TB == 0:
                        o_evacuate(v // TB - 1)
                    exp(v + 1, 0)
                    read_misc(b, use, ix, (4 * u, 4 * u + 1))
                    exp(v + 1, 1)
                    read_misc(b, use, ix, (4 * u + 2, 4 * u + 3))

            for s in range(2):
                act.wait_ge(parts_out[s], 16 * 2 * B)
            for n in range(4 * NCH):
                c, gap = divmod(n, 4)
                if gap < IC:
                    act.wait_ge(sh_gu, c * IC + gap + 1)
                    nc.scalar.activation(TH[:, gap, :], PS[:, gap, :], ACT.Tanh, scale=0.5).then_inc(sh_th, 1)
                read_misc(None, PRE_USE, PRE_IX, (n,))
            act.wait_ge(sh_h, NCH * IC)
            act.wait_ge(sh_y, NCH - 1)
            exp(0, 0)
            exp(0, 1)
            for b in range(B):
                batch(b, USE[b], IX[b])
            o_evacuate(B * NJ - 1)

        @block.vector
        def _(dve):
            o = Steps(dve, dve_steps)
            o.done(nc.vector.memset(WQKV[:, :, :], 0.0))

            def moments(src, s):
                for j in range(TC):
                    last = nc.vector.bn_stats(ST[:, s, j, :], src(j))
                o.done(last)
                for j in range(TC):
                    last = nc.vector.bn_aggr(MV[:, s, j, :], ST[:, s, j, :])
                o.done(last)
                nc.vector.tensor_scalar(RSTD[:, s, :], MV[:, s, :, 1], EPS, None, ALU.add).then_inc(var_done, 1)

            def normalize(src, dst, s):
                for j in range(TC):
                    last = nc.vector.tensor_scalar(dst(j), src(j), MV[:, s, j, 0:1], RSTD[:, s, j:j + 1],
                                                   ALU.subtract, ALU.mult)
                return last

            x_tile = lambda c: lambda j: RES[:, c * TC + j, :]
            xn_tile = lambda c: lambda j: XN[:, c % 2, j, :]

            def x_moments(c):
                dve.wait_ge(x_in[c % 2], 16 * (c // 2 + 1))
                moments(x_tile(c), c % 2)

            def place_projections():
                dve.wait_ge(wqkv_ps, 1)
                for g in range(G):
                    half = slice(g * HG * DH, (g + 1) * HG * DH)
                    last = nc.vector.tensor_copy(WQKV[half, :, half],
                                                 PS[half, 7, 0:3 * HG * DH].rearrange("p (k d) -> p k d", k=3))
                last.then_inc(wqkv_ready, 1)

            x_moments(0)
            for n in range(NCH + 2):
                if n + 1 < NCH:
                    x_moments(n + 1)
                if n == 1:
                    place_projections()
                if n < NCH:
                    dve.wait_ge(rstd_done, 2 * n if n else 1)
                    if n >= 2:
                        dve.wait_ge(xnT_ps, n - 1)
                        dve.wait_ge(res_done, n - 1)
                        dve.wait_ge(z_done, n - 1)
                    normalize(x_tile(n), xn_tile(n), n % 2).then_inc(xn_done, 1)
                    dve.wait_ge(xn_done, n + 1)
                    moments(xn_tile(n), 2 + n % 2)
                if 1 <= n <= NCH:
                    z = n - 1
                    dve.wait_ge(rstd_done, min(2 * z + 3, 2 * NCH))
                    normalize(xn_tile(z), lambda j: ZALL[:, z * TC + j, 0:D], 2 + z % 2).then_inc(z_done, 1)
                if n >= 2:
                    q = n - 2
                    dve.wait_ge(qk_ev, q + 1)
                    nc.vector.tensor_tensor(QF[:, q % 2], QF[:, q % 2], PARTS[:, q % 2, :, 0, :], ALU.subtract).then_inc(rest_done, 1)
                    dve.wait_ge(qkv_ps, q + 1)
                    for j in range(TC):
                        last = nc.vector.tensor_tensor(
                            VALL[:, q * TC + j, :, 0:DH],
                            PS[:, 4 + q % 2, j * D:(j + 1) * D].rearrange("p (h d) -> p h d", h=H),
                            BVR[:, :].rearrange("p (h d) -> p h d", h=H), ALU.add)
                    last.then_inc(v_ev, 1)

            def row_max(first, slot, row, j):
                dve.wait_ge(a_ps, first + (j + 1))
                nc.vector.tensor_reduce(MXP[:, slot, row, j % 2:j % 2 + 1], PS[:, 4 + j % 2, :], AX.X, ALU.max).then_inc(a_max, 1)

            def block(b, n):
                ahead, j = divmod(n if b is None else n + 4 * (QUADS + LEAD), 4 * QUADS)
                b = b or 0
                first = (2 * b + ahead) * (4 * QUADS)
                row_max(first, ahead % 2, j // 2, j)
                if j == 4 * QUADS - 1:
                    finalize(b * 2 + ahead, ahead % 2)

            def finalize(i, slot):
                dve.wait_ge(a_max, (i + 1) * (4 * QUADS))
                if i >= 2:
                    dve.wait_ge(nm_in, (i - 1) * (16 * NPART))
                o.done(nc.vector.tensor_reduce(NMF[:, slot, :], MXP[:, slot, :, :], AX.X, ALU.max, negate=True))
                rest = NMF[:, slot, :].rearrange("p (h t) -> p t h", h=HG)
                for a in range(NPART):
                    part = NMP[:, slot, :, a, :]
                    ins = nc.vector.tensor_copy(part, rest)
                    if a < NPART - 1:
                        o.done(ins)
                        o.done(nc.vector.tensor_tensor(rest, rest, part, ALU.subtract))
                ins.then_inc(nm_done, 1)

            for m in range(ROUTE_BLOCKS // 2):
                block(None, m)
            per_t = lambda v: v.unsqueeze(2).to_broadcast([P, NT, E])
            dve.wait_ge(lg_ps, NCH)
            dve.wait_ge(consts, 3)
            o.done(nc.vector.tensor_copy(LG[:, :, :], PS[:, 6, 0:NT * E].rearrange("p (t e) -> p t e", t=NT)))
            nc.vector.tensor_reduce(MXL[:, :], LG[:, :, :], AX.X, ALU.max).then_inc(mxl_done, 1)
            dve.wait_ge(mxl_done, 1)
            o.done(nc.vector.tensor_tensor(OH[:, :, :], LG[:, :, :], per_t(MXL[:, :]), ALU.is_equal))
            o.done(nc.vector.tensor_tensor(OH[:, :, :], OH[:, :, :], PREF[:, :, :], ALU.mult))
            o.done(nc.vector.tensor_reduce(DST[:, :], OH[:, :, :], AX.X, ALU.max))
            nc.vector.tensor_tensor(OH[:, :, :], OH[:, :, :], per_t(DST[:, :]), ALU.is_equal).then_inc(oh_done, 1)
            for m in range(ROUTE_BLOCKS // 2, ROUTE_BLOCKS):
                block(None, m)
            dve.wait_ge(tanh_done, 1)
            o.done(nc.vector.tensor_scalar(SCO[:, 0, :], SCO[:, 0, :], 0.5, 0.5, ALU.mult, ALU.add))
            nc.vector.tensor_scalar(ZALL[:, :, D], SCO[:, 0, :], 0.5, None, ALU.mult)
            o.done(nc.vector.scalar_tensor_tensor(ZALL[:, :, D + 1], SCO[:, 0, :], 0.5, SCO[:, 0, :], ALU.mult, ALU.mult))
            per_e = lambda v: v.unsqueeze(2).to_broadcast([P, E, NT])
            flat = lambda T: T[:, :, :].rearrange("p a b -> p (a b)")
            dve.wait_ge(rank_ps, 1)
            o.done(nc.vector.tensor_copy(TOT[:, :, :], PS[:, 7, 0:NT * E].rearrange("p (t e) -> p e t", t=NT)))
            o.done(nc.vector.tensor_tensor_scan(flat(INC), flat(TOT), ZER[:, :], 0.0, ALU.add, ALU.add))
            o.done(nc.vector.tensor_tensor(CNT[:, :], INC[:, :, NT - 1], INC[:, :, 0], ALU.subtract))
            o.done(nc.vector.tensor_tensor(CNT[:, :], CNT[:, :], TOT[:, :, 0], ALU.add))
            more = LG[:, :, :].rearrange("p t e -> p (t e)").rearrange("p (e t) -> p e t", e=E)
            o.done(nc.vector.tensor_tensor(more, per_e(CNT[:, :]), T128[:, :, :], ALU.is_gt))
            o.done(nc.vector.tensor_reduce(NTE[:, :], more, AX.X, ALU.add))
            o.done(nc.vector.tensor_tensor_scan(ENDT[:, :], NTE[:, :], ZER[:, 0:E], 0.0, ALU.add, ALU.add))
            o.done(nc.vector.tensor_tensor(NTE[:, :], ENDT[:, :], NTE[:, :], ALU.subtract))
            o.done(nc.vector.tensor_tensor(CNT[:, :], TOT[:, :, 0], INC[:, :, 0], ALU.subtract))
            o.done(nc.vector.scalar_tensor_tensor(BASE[:, :], NTE[:, :], float(P), CNT[:, :], ALU.mult, ALU.add))
            o.done(nc.vector.tensor_tensor(INC[:, :, :], INC[:, :, :], TOT[:, :, :], ALU.subtract))
            o.done(nc.vector.tensor_tensor(INC[:, :, :], INC[:, :, :], per_e(BASE[:, :]), ALU.add))
            o.done(nc.vector.tensor_tensor(LG[:, :, :], PS[:, 6, 0:NT * E].rearrange("p (t e) -> p t e", t=NT),
                                           INC[:, :, :].rearrange("p e t -> p t e"), ALU.add))
            o.done(nc.vector.tensor_tensor(LG[:, :, :], LG[:, :, :], OH[:, :, :], ALU.mult))
            o.done(nc.vector.tensor_reduce(DST[:, :], LG[:, :, :], AX.X, ALU.add))
            nc.vector.tensor_copy(DSTI[:, :], DST[:, :]).then_inc(place_done, 1)
            o.done(nc.vector.tensor_tensor(TIDX[:, :, :], TIDX[:, :, :],
                                           ENDT[:, :].unsqueeze(1).to_broadcast([P, NS, E]), ALU.is_ge))
            o.done(nc.vector.tensor_reduce(TEF[:, :], TIDX[:, :, :], AX.X, ALU.add))
            nc.vector.tensor_scalar(TEI[:, :], TEF[:, :], float(E - 1), None, ALU.min).then_inc(tile_expert, 1)

            dve.wait_ge(res_done, NCH)
            def hidden(c, i):
                dve.wait_ge(sh_th, c * IC + i + 1)
                if c >= 2:
                    dve.wait_ge(sh_y, c - 1)
                o.done(nc.vector.scalar_tensor_tensor(HID[:, c % 2, i, :], TH[:, i, :], 1.0, PS[:, i, :], ALU.add, ALU.mult))
                nc.vector.scalar_tensor_tensor(HID[:, c % 2, i, :], HID[:, c % 2, i, :], 0.5, PS[:, IC + i, :], ALU.mult,
                                               ALU.mult).then_inc(sh_h, 1)

            def add_shared(c):
                dve.wait_ge(sh_y, c + 1)
                t = slice(c * TC, (c + 1) * TC)
                nc.vector.tensor_tensor(RES[:, t, :], RES[:, t, :], PS[:, 6, :].rearrange("p (t d) -> p t d", t=TC),
                                        ALU.add).then_inc(sh_add, 1)

            def tile_hidden(b, k):
                s = tile(b, k) % 2
                dve.wait_ge(tile_th, tile(b, k) + 1)
                o.done(nc.vector.scalar_tensor_tensor(HR[:, s, :], THR[:, s, :], 1.0, PS[:, 7, 0:I], ALU.add, ALU.mult))
                nc.vector.scalar_tensor_tensor(HR[:, s, :], HR[:, s, :], XS[:, s, D + 1:D + 2], PS[:, 7, I:2 * I], ALU.mult,
                                               ALU.mult).then_inc(misc_read, 1)

            def output(b, j, ix):
                g, qh = divmod(j % NJ, 2)
                if j == (B - 1) * NJ:
                    dve.wait_ge(routed_add, 1)
                dve.wait_ge(misc_ps, misc(b, ix["out", j] + 1))
                o_t = PS[:, 7, :].rearrange("p (t h m) -> p t h m", t=TC, h=HG)
                o.done(nc.vector.reciprocal(REC[:, :, :], o_t[:, :, :, DH]))
                nc.vector.tensor_tensor(OTM[:, :, :, :], o_t[:, :, :, 0:DH],
                                        REC[:, :, :].unsqueeze(3).to_broadcast([P, TC, HG, DH]), ALU.mult).then_inc(misc_read, 1)
                dve.wait_ge(misc_read, misc(b, ix["out", j] + 1))
                t0 = j // NJ * TB + qh * TC
                dst = RES[:, t0:t0 + TC, g * HG * DH:(g + 1) * HG * DH]
                nc.vector.tensor_tensor(dst, dst, OTM[:, :, :, :].rearrange("p t h d -> p t (h d)"),
                                        ALU.add).then_inc(o_done, 1)

            def batch(b, last, use, ix):
                for n in range(4 * UPB):
                    if not last or n + 4 * (QUADS + LEAD) < 8 * QUADS:
                        block(b, n)
                    kind, k = use.get(n - HID_AFTER, (None, None))
                    if kind == "gu":
                        tile_hidden(b, k)
                    if kind == "out":
                        output(b, k, ix)

            for n in range(4 * NCH):
                c, gap = divmod(n, 4)
                for m in pre_blocks(n):
                    block(None, m)
                if gap < IC:
                    hidden(c, gap)
                if gap == 3 and c:
                    add_shared(c - 1)
                kind, k = PRE_USE.get(n - 1, (None, None))
                if kind == "gu":
                    tile_hidden(None, k)
            add_shared(NCH - 1)
            for b in range(B):
                batch(b, b == B - 1, USE[b], IX[b])
            output(B - 1, B * NJ - 1, IX[B - 1])

        @block.tensor
        def _(pe):
            mm = nc.tensor.matmul
            pe.wait_ge(consts, 2)

            def project_factors():
                pe.wait_ge(fac_bd, 1)
                GD = HG * DH
                for k in range(3):
                    for g in range(G):
                        last = mm(PS[g * GD:(g + 1) * GD, 7, k * GD:(k + 1) * GD],
                                  FACBD[:, k, 0, g].rearrange("p j d -> p (j d)"),
                                  FACBD[:, k, 1, g].rearrange("p j d -> p (j d)"), start=True, stop=True)
                last.then_inc(wqkv_ps, 1)

            def block_of_scores(par, head, j, first):
                qt, kh = j // 2 % TB, j % 2
                if first + j >= 2:
                    pe.wait_ge(a_max, first + j - 1)
                mm(PS[:, 4 + kh, :], QS[0:KR, par, head, qt * P:(qt + 1) * P],
                   KS[0:KR, par, head, kh * CH:(kh + 1) * CH], start=True, stop=True).then_inc(a_ps, 1)

            def block(b, n):
                ahead, j = divmod(n if b is None else n + 4 * (QUADS + LEAD), 4 * QUADS)
                b = b or 0
                first = (2 * b + ahead) * (4 * QUADS)
                if ahead % 2 == 0 and j == 0:
                    pe.wait_ge(stack_in, (b + ahead // 2 + 1) * (16 * N_STACK))
                par = (b + ahead // 2) % 2
                block_of_scores(par, ahead % 2 * HG + j // (2 * TB), j, first)

            def logits(c):
                pe.wait_ge(xfT_ev, c + 1)
                for t in range(c * TC, (c + 1) * TC):
                    last = mm(PS[:, 6, t * E:(t + 1) * E], XFT[:, t * P:(t + 1) * P], RW[:, :], start=True, stop=True)
                last.then_inc(lg_ps, 1)

            for n in range(NCH + 1):
                s, z = n % 2, n - 1
                if n < NCH:
                    pe.wait_ge(xn_done, n + 1)
                    if n:
                        pe.wait_ge(xnT_ev, n)
                    for j in range(TC):
                        last = nc.tensor.transpose(PS[:, 0, j * P:(j + 1) * P], XN[:, s, j, :], IDF[:, :])
                    last.then_inc(xnT_ps, 1)
                if n == 0:
                    project_factors()
                    pe.wait_ge(wqkv_ready, 1)
                if n:
                    pe.wait_ge(xnT_ev, n)
                    if n >= 2:
                        pe.wait_ge(qk_ev, n - 1)
                    if n >= 3:
                        pe.wait_ge(v_ev, n - 2)
                    for k in range(2):
                        mm(PS[:, 2 + k, :], WQKV[:, k, :], XNT[:, z % 2, :], start=True, stop=True)
                    for j in range(TC):
                        last = mm(PS[:, 4 + z % 2, j * D:(j + 1) * D], XNT[:, z % 2, j * P:(j + 1) * P], WQKV[:, 2, :],
                                  start=True, stop=True)
                    last.then_inc(qkv_ps, 1)
                if n >= 2:
                    logits(n - 2)
                if n:
                    pe.wait_ge(z_done, n)
                    if n >= 2:
                        pe.wait_ge(xfT_ev, n - 1)
                    for j in range(TC):
                        last = nc.tensor.transpose(PS[:, 1, j * P:(j + 1) * P], ZALL[:, z * TC + j, 0:D], IDF[:, :])
                    last.then_inc(zT_ps, 1)
            pe.wait_ge(v_ev, NCH)
            block(None, 0)
            block(None, 1)
            logits(NCH - 1)
            for m in range(2, ROUTE_BLOCKS // 2):
                block(None, m)

            pe.wait_ge(oh_done, 1)
            hot = OH[:, :, :].rearrange("p t e -> p (t e)")
            mm(PS[:, 6, 0:NT * E], TRI[:, :], hot, start=True, stop=True)
            mm(PS[:, 7, 0:NT * E], ONE[:, :], hot, start=True, stop=True).then_inc(rank_ps, 1)
            for m in range(ROUTE_BLOCKS // 2, ROUTE_BLOCKS):
                block(None, m)

            def gate_up(c, i):
                if c:
                    pe.wait_ge(sh_h, (c - 1) * IC + i + 1)
                for j in (i, IC + i):
                    last = mm(PS[:, j, :], SHGU[:, j * P:(j + 1) * P], XFT[:, c * CH:(c + 1) * CH], start=True, stop=True)
                last.then_inc(sh_gu, 1)

            def down(c):
                pe.wait_ge(sh_h, (c + 1) * IC)
                if c:
                    pe.wait_ge(sh_add, c)
                for j in range(TC):
                    for i in range(IC):
                        last = mm(PS[:, 6, j * D:(j + 1) * D], HID[:, c % 2, i, j * P:(j + 1) * P], SHD[:, i, :],
                                  start=(i == 0), stop=(i == IC - 1))
                last.then_inc(sh_y, 1)

            experts = {}

            def load_expert(t):
                if t < NS:
                    experts[t] = pe.value_load(TEI[0:1, t:t + 1], min_val=0, max_val=E - 1)

            def write_misc(b, use, ix, n):
                if n not in use:
                    return
                kind, k = use[n]
                s = tile(b, k) % 2
                if b is not None or ix[kind, k]:
                    pe.wait_ge(misc_read, misc(b, ix[kind, k]))
                if kind == "yx":
                    if b is not None or k:
                        expert = experts.pop(tile(b, k) - 1)
                        for i in range(IC):
                            mm(PS[:, 7, 0:D], HRT[:, 1 - s, i * P:(i + 1) * P], WD[:, expert, i, :],
                               start=(i == 0), stop=(i == IC - 1))
                    pe.wait_ge(xs_in[s], (tile(b, k) // 2 + 1) * 16)
                    last = nc.tensor.transpose(PS[:, 7, D:D + P], XS[:, s, 0:D], IDF[:, :])
                if kind == "gu":
                    mm(PS[:, 7, :], XET[:, s, :], WGU[:, experts[tile(b, k)], :], start=True, stop=True).then_inc(misc_ps, 1)
                    load_expert(tile(b, k) + 1)
                    return
                if kind == "ht":
                    for i in range(IC):
                        last = nc.tensor.transpose(PS[:, 7, i * P:(i + 1) * P], HR[:, s, i * P:(i + 1) * P], IDF[:, :])
                if kind == "nm":
                    pe.wait_ge(nm_done, (0 if b is None else b * 2) + (k + 1))
                    rows = PS[0:NPART * HG, 7, :].bitcast(BF16)
                    for t in range(TB):
                        last = nc.tensor.transpose(rows[:, t * P:(t + 1) * P],
                                                   NMP[:, k % 2, t].rearrange("p a h -> p (a h)"), IDB[:, :])
                if kind == "out":
                    pe.wait_ge(o_ev, k + 1)
                    for t in range(TC):
                        last = nc.tensor.transpose(PS[:, 7, t * P:(t + 1) * P], OSB[:, t * P:(t + 1) * P], IDF[:, :])
                last.then_inc(misc_ps, 1)

            def scores(b, u, hp):
                b, u = b + u // UPB, u % UPB
                if b == B:
                    return
                g, qh, kt = u // (2 * TB), u // TB % 2, u % TB
                if qh == 0 and kt == 0 and hp == 0:
                    pe.wait_ge(nm_in, b * (2 * 16 * NPART) + ((g + 1) * (16 * NPART)))
                if b or u:
                    pe.wait_ge(p_done, b * (2 * UPB) + (2 * u + hp - 1))
                for j in range(2):
                    head = g * HG + 2 * hp + j
                    last = mm(PS[:, 2 * hp + j, :], KS[0:KM, b % 2, head, kt * P:(kt + 1) * P],
                              QS[0:KM, b % 2, head, qh * CH:(qh + 1) * CH], start=True, stop=True)
                last.then_inc(s_ps, 1)

            def values(b, u, part):
                g, qh, kt = u // (2 * TB), u // TB % 2, u % TB
                q = slice(part * (CH // 2), (part + 1) * (CH // 2))
                if part == 0:
                    if kt == 0 and b * 4 + u // TB:
                        pe.wait_ge(o_ev, b * 4 + u // TB)
                    if kt == 0 and qh == 0:
                        pe.wait_ge(vst_done, b * G + (g + 1))
                    pe.wait_ge(p_done, b * (2 * UPB) + (2 * u + 2))
                for j in range(HG):
                    last = mm(PS[j * VM:(j + 1) * VM, 6, q], VST[:, g, kt, j, :], PR[:, (u % 2) * 2 + j // 2, j % 2, q],
                              start=(kt == 0 and part == 0), stop=(kt == TB - 1 and part == 1))
                if part == 1:
                    last.then_inc(pv_done, 1)

            def batch(b, last, use, ix):
                for u in range(UPB):
                    for gap in range(4):
                        n = 4 * u + gap
                        if not last or n + 4 * (QUADS + LEAD) < 8 * QUADS:
                            block(b, n)
                        if gap < 2:
                            scores(b, u + 1, gap)
                        else:
                            values(b, u, gap - 2)
                        write_misc(b, use, ix, n)

            pe.wait_ge(w2_in, 16 * N_W2)
            for n in range(4 * NCH):
                c, gap = divmod(n, 4)
                if gap < IC:
                    gate_up(c, gap)
                if gap == 2 and c == 1:
                    pe.wait_ge(place_done, 1)
                if n == PRE_AT[0]:
                    pe.wait_ge(w3_in, 16 * N_W3)
                    pe.wait_ge(tile_expert, 1)
                    load_expert(0)
                if gap == 2 and c:
                    down(c - 1)
                for m in pre_blocks(n):
                    block(None, m)
                write_misc(None, PRE_USE, PRE_IX, n)
            down(NCH - 1)
            pe.wait_ge(ones_in, 16)
            pe.wait_ge(sh_h, NCH * IC)
            scores(0, 0, 0)
            scores(0, 0, 1)
            pe.wait_ge(sh_add, NCH)
            for b in range(B):
                batch(b, b == B - 1, USE[b], IX[b])
            write_misc(B - 1, USE[B - 1], IX[B - 1], 4 * UPB)


_INS = ["x", "Uq", "Vq", "bq", "Uk", "Vk", "bk", "Uv", "Vv", "bv", "ln_w", "ln_b", "router_w",
        "gate_w", "up_w", "down_w", "sh_gate", "sh_up", "sh_down"]


def kernel(**inputs):
    import numpy as _np
    import concourse.bacc as _bacc
    from concourse import mybir as _mybir
    from concourse.bass_utils import run_bass_kernel_spmd as _run

    nc = _bacc.Bacc("TRN2", target_bir_lowering=False, num_devices=1)
    arrays, args = {}, []
    for name in _INS:
        full = next(k for k in inputs if k in (f"L0_attn_{name}", f"L0_ffn_{name}"))
        a = _np.asarray(inputs[full])
        if name in ("Uq", "Uk", "Uv"):
            a = a.transpose(0, 2, 1)
        a = _np.ascontiguousarray(a)
        arrays[f"in_{name}_dram"] = a
        args.append(nc.dram_tensor(f"in_{name}_dram", a.shape, _mybir.dt.from_np(a.dtype), kind="ExternalInput").ap())
    dt = _mybir.dt.from_np(_np.dtype("float32"))
    args.append(nc.dram_tensor("out_0_dram", (4, 1024, 128), dt, kind="ExternalOutput").ap())
    build_kernel(nc, *args)
    r = _run(nc, [arrays], core_ids=[0])
    return r.results[0]["out_0_dram"]
```
